# Optimizing a Trainium2 kernel written in Bass

```python
import numpy as np
import jax
import jax.numpy as jnp

def _softmax(x, axis=-1):
    return jax.nn.softmax(x, axis=axis)

def _gelu(x):
    return jax.nn.gelu(x, approximate=True)

def _silu(x):
    return jax.nn.silu(x)

def _sigmoid(x):
    return jax.nn.sigmoid(x)

def _layernorm(x, axis=-1, eps=1e-05):
    m = jnp.mean(x, axis=axis, keepdims=True)
    v = jnp.var(x, axis=axis, keepdims=True)
    return (x - m) / jnp.sqrt(v + eps)

def _scatter_add(tgt, idx, src, axis=0):
    return tgt.at[idx].add(src)

def _segment_sum(src, seg, n):
    return jax.ops.segment_sum(src, seg, n)
kernel_name = 'mk_gnn_preln_d2_gnn_r64_0ac7a0'

def setup_inputs(seed: int=0):
    np.random.seed(seed)
    _w = jnp.asarray

    def _rec_inputs():
        import jax
        import jax.numpy as jnp
        _gk = jax.random.key(seed)
        x = -6.415e-05 + 1 * jax.random.normal(jax.random.fold_in(_gk, 1), (10000, 512), jnp.float32)
        src = jax.random.randint(jax.random.fold_in(_gk, 2), (5000,), 0, 10000, jnp.int32)
        dst = jnp.minimum((10000 * jax.random.uniform(jax.random.fold_in(_gk, 3), (5000,)) ** 2.0).astype(jnp.int32), 9999)
        _o = jnp.argsort(dst, stable=True)
        src = src[_o]
        dst = dst[_o]
        edge_type_8 = jax.random.randint(jax.random.fold_in(_gk, 13), (5000,), 0, 8, jnp.int32)
        edge_weight = jax.random.uniform(jax.random.fold_in(_gk, 14), (5000,), jnp.float32, 0.0, 0.999998)
        return (x, src, dst, edge_type_8, edge_weight)
    x, src, dst, edge_type_8, edge_weight = _rec_inputs()

    def _L0_gnn_setup():
        import jax, jax.numpy as jnp
        import numpy as np
        N_NODES = 20000
        N_EDGES = 5000
        D = 512
        NUM_RELS = 8
        NUM_BASES = 4

        def _rel_graph_conv(h, src, dst, etypes, norm, basis, comp, bias, loop_w, apply_relu):
            n = h.shape[0]
            hb = jnp.einsum('nd,bdo->bno', h, basis)
            coef = comp[etypes]
            m = coef[:, 0, None] * hb[0][src]
            for b in range(1, basis.shape[0]):
                m = m + coef[:, b, None] * hb[b][src]
            m = m * norm[:, None]
            agg = jax.ops.segment_sum(m, dst, num_segments=n)
            out = agg + bias + h @ loop_w
            if apply_relu:
                out = jax.nn.relu(out)
            return out
        key = jax.random.key(seed)
        ks = jax.random.split(key, 16)
        inp = {'emb': jax.random.normal(ks[0], (N_NODES, D), dtype=jnp.float32), 'src': jax.random.randint(ks[1], (N_EDGES,), 0, N_NODES), 'dst': jax.random.randint(ks[2], (N_EDGES,), 0, N_NODES), 'etypes': jax.random.randint(ks[3], (N_EDGES,), 0, NUM_RELS), 'edge_norm': jax.random.uniform(ks[4], (N_EDGES,), dtype=jnp.float32)}
        s = 1.0 / np.sqrt(D)
        inp['basis0'] = jax.random.normal(ks[5], (NUM_BASES, D, D), dtype=jnp.float32) * s
        inp['comp0'] = jax.random.normal(ks[6], (NUM_RELS, NUM_BASES), dtype=jnp.float32)
        inp['bias0'] = jnp.zeros((D,), dtype=jnp.float32)
        inp['loop0'] = jax.random.normal(ks[7], (D, D), dtype=jnp.float32) * s
        inp['basis1'] = jax.random.normal(ks[8], (NUM_BASES, D, D), dtype=jnp.float32) * s
        inp['comp1'] = jax.random.normal(ks[9], (NUM_RELS, NUM_BASES), dtype=jnp.float32)
        inp['bias1'] = jnp.zeros((D,), dtype=jnp.float32)
        inp['loop1'] = jax.random.normal(ks[10], (D, D), dtype=jnp.float32) * s
        return inp
    _L0_gnn_all = _L0_gnn_setup()
    _L0_gnn_in = {k: v for k, v in _L0_gnn_all.items() if k in ('basis0', 'comp0', 'bias0', 'loop0', 'basis1', 'comp1', 'bias1', 'loop1')}
    del _L0_gnn_all

    def _L1_gnn_setup():
        import jax, jax.numpy as jnp
        import numpy as np
        N_NODES = 50000
        N_EDGES = 6250
        IN_DIM = 512
        OUT_DIM = 512
        key = jax.random.key(seed)
        k1, k2, k3, k4 = jax.random.split(key, 4)
        x = jax.random.normal(k1, (N_NODES, IN_DIM), dtype=jnp.float32)
        edge_index = jax.random.randint(k2, (2, N_EDGES), 0, N_NODES, dtype=jnp.int64)
        W = jax.random.normal(k3, (OUT_DIM, IN_DIM), dtype=jnp.float32) / np.sqrt(IN_DIM)
        b = jax.random.normal(k4, (OUT_DIM,), dtype=jnp.float32) * 0.01
        return {'x': x, 'edge_index': edge_index, 'W': W, 'b': b}
    _L1_gnn_all = _L1_gnn_setup()
    _L1_gnn_in = {k: v for k, v in _L1_gnn_all.items() if k in ('W', 'b')}
    del _L1_gnn_all
    return {'x': x, 'src': src, 'dst': dst, 'edge_type_8': edge_type_8, 'edge_weight': edge_weight, 'L0_gnn_basis0': _L0_gnn_in['basis0'], 'L0_gnn_comp0': _L0_gnn_in['comp0'], 'L0_gnn_bias0': _L0_gnn_in['bias0'], 'L0_gnn_loop0': _L0_gnn_in['loop0'], 'L0_gnn_basis1': _L0_gnn_in['basis1'], 'L0_gnn_comp1': _L0_gnn_in['comp1'], 'L0_gnn_bias1': _L0_gnn_in['bias1'], 'L0_gnn_loop1': _L0_gnn_in['loop1'], 'L1_gnn_W': _L1_gnn_in['W'], 'L1_gnn_b': _L1_gnn_in['b']}

def reference(x, src, dst, edge_type_8, edge_weight, L0_gnn_basis0, L0_gnn_comp0, L0_gnn_bias0, L0_gnn_loop0, L0_gnn_basis1, L0_gnn_comp1, L0_gnn_bias1, L0_gnn_loop1, L1_gnn_W, L1_gnn_b):
    import jax
    import jax.numpy as jnp

    def _L0_gnn_ref(emb, src, dst, etypes, edge_norm, basis0, comp0, bias0, loop0, basis1, comp1, bias1, loop1):
        import jax, jax.numpy as jnp
        import numpy as np
        N_NODES = 20000
        N_EDGES = 5000
        D = 512
        NUM_RELS = 8
        NUM_BASES = 4

        def _rel_graph_conv(h, src, dst, etypes, norm, basis, comp, bias, loop_w, apply_relu):
            n = h.shape[0]
            hb = jnp.einsum('nd,bdo->bno', h, basis)
            coef = comp[etypes]
            m = coef[:, 0, None] * hb[0][src]
            for b in range(1, basis.shape[0]):
                m = m + coef[:, b, None] * hb[b][src]
            m = m * norm[:, None]
            agg = jax.ops.segment_sum(m, dst, num_segments=n)
            out = agg + bias + h @ loop_w
            if apply_relu:
                out = jax.nn.relu(out)
            return out
        h = _rel_graph_conv(emb, src, dst, etypes, edge_norm, basis0, comp0, bias0, loop0, True)
        h = _rel_graph_conv(h, src, dst, etypes, edge_norm, basis1, comp1, bias1, loop1, False)
        return h

    def _L1_gnn_ref(x, edge_index, W, b):
        import jax, jax.numpy as jnp
        import numpy as np
        N_NODES = 50000
        N_EDGES = 6250
        IN_DIM = 512
        OUT_DIM = 512
        n = x.shape[0]
        loops = jnp.arange(n, dtype=edge_index.dtype)
        row = jnp.concatenate([edge_index[0], loops])
        col = jnp.concatenate([edge_index[1], loops])
        deg = jax.ops.segment_sum(jnp.ones(row.shape[0], dtype=x.dtype), row, num_segments=n)
        dis = jax.lax.rsqrt(deg)
        norm = dis[row] * dis[col]
        h = x @ W.T + b
        out = jax.ops.segment_sum(norm[:, None] * h[row], col, num_segments=n)
        return jax.nn.relu(out)
    edge_index = jnp.stack([src, dst])
    h = jnp.maximum(_layernorm(x, axis=-1), 0.0)
    x = x + _L0_gnn_ref(h, src, dst, edge_type_8, edge_weight, L0_gnn_basis0, L0_gnn_comp0, L0_gnn_bias0, L0_gnn_loop0, L0_gnn_basis1, L0_gnn_comp1, L0_gnn_bias1, L0_gnn_loop1)
    h = jnp.maximum(_layernorm(x, axis=-1), 0.0)
    x = x + _L1_gnn_ref(h, edge_index, L1_gnn_W, L1_gnn_b)
    return x

_drawn_inputs = setup_inputs


def setup_inputs(seed=0):
    import zlib

    import numpy as np

    out = dict(_drawn_inputs(seed))
    spreads = {'L0_gnn_bias0': (0.0, 0.1), 'L0_gnn_bias1': (0.0, 0.1)}
    factors = {'L1_gnn_b': 8.0}
    for name, (base, spread) in spreads.items():
        noise = np.random.default_rng([zlib.crc32(name.encode()), seed]).standard_normal(out[name].shape)
        drawn = base * np.exp(spread * noise) if base else spread * noise
        out[name] = jnp.asarray(drawn.astype(out[name].dtype))
    for name, factor in factors.items():
        out[name] = (out[name] * factor).astype(out[name].dtype)
    return out
```

```python
from contextlib import ExitStack

import concourse.bass as bass
from concourse import mybir

P = 128
ALU = mybir.AluOpType
ACT = mybir.ActivationFunctionType
F32 = mybir.dt.float32
F16 = mybir.dt.float16
I32 = mybir.dt.int32
AX_X = mybir.AxisListType.X
EPS = 1e-5
SCALE = 64.0


def wait(eng, sem, value):
    if not isinstance(value, int) or value > 0:
        eng.wait_ge(sem, value)


def inside(t, count):
    return not isinstance(t, int) or 0 <= t < count


def steps(eng, tiles, unroll, lead, step):
    for k in range(-lead, unroll):
        step(0, k)
    with eng.Fori(1, tiles // unroll - 1) as i:
        for k in range(unroll):
            step(i, k)
    for k in range(unroll):
        step(tiles // unroll - 1, k)


class NodePass:

    def __init__(self, number, tile0, evac0, norm0=None, ln0=None, unit0=None):
        self.number, self.tile0, self.evac0 = number, tile0, evac0
        self.norm0, self.ln0, self.unit0 = norm0, ln0, unit0


class EdgePass:

    def __init__(self, number, tile0, evac0, norm0, ln0=None, unit0=None):
        self.number, self.tile0, self.evac0 = number, tile0, evac0
        self.norm0, self.ln0, self.unit0 = norm0, ln0, unit0


def gnn_kernel(nc, x, src, dst, etype, weight, basis0, comp0, bias0, loop0,
               basis1, comp1, bias1, loop1, w2t, bias2, out):
    N, D = x.shape
    E = src.shape[0]
    R, B = comp0.shape
    KC = D // P
    NT = 80
    NP = N // NT
    GT = 2
    U = 8
    XS, OS = 4, 2
    EC = 40
    EP = E // EC
    ET = -(-((E + R * (P - 1)) // P) // U) * U
    GS, MS = 4, 4
    WIDE = D + 4
    ROWS = N + P
    FULL = NP // 16 * 16
    ZB, ZT = 5, 25
    WB = 6 * KC
    assert NP * NT == N and EP * EC == E and NP <= P and EP <= P and ET == 48 and R == NT // U - 2

    acc1 = nc.dram_tensor("acc1", (ROWS, D), F32, kind="Internal").ap()
    acc2 = nc.dram_tensor("acc2", (ROWS, WIDE), F32, kind="Internal").ap()
    acc3 = nc.dram_tensor("acc3", (ROWS, D), F32, kind="Internal").ap()

    A = NodePass(0, 0, 0, norm0=0, ln0=0, unit0=0)
    Bp = EdgePass(0, NT, 0, norm0=NT, ln0=NT, unit0=NT // GT)
    C = NodePass(1, NT + ET, NT)
    Dp = EdgePass(1, 2 * NT + ET, ET, norm0=NT + ET)
    Fp = EdgePass(2, 2 * NT + 2 * ET, 2 * NT, norm0=NT + 2 * ET, ln0=NT + ET, unit0=NT // GT + ET)
    Z = NodePass(2, 2 * NT + 3 * ET, 2 * NT + ET, norm0=NT + 3 * ET, ln0=NT + 2 * ET, unit0=NT // GT + 2 * ET)

    with ExitStack() as ctx:
        def sb(name, shape, dt):
            return ctx.enter_context(nc.sbuf_tensor(name, shape, dt))

        def psum(name, shape):
            return ctx.enter_context(nc.psum_tensor(name, shape, F32))

        def sem(name):
            return ctx.enter_context(nc.semaphore(name))

        rel_w = sb("rel_w", [P, R * 2 * KC * D], F16)
        node_w = [sb(f"node_w{n}", [P, 2, KC, D], F16) for n in range(2)]
        basis = sb("basis", [P, B, KC, D], F32)
        combined = sb("combined", [P, D], F32)
        comp = [sb(f"comp{n}", [P, R * B], F32) for n in range(2)]
        bias = [sb(f"bias{n}", [P, D], F32) for n in range(3)]
        bias_rows = basis[:, 1, 0:2, :]
        xring = sb("xring", [P, XS, GT, WIDE], F32)
        gring = sb("gring", [P, XS, GT, D], F32)
        oring = sb("oring", [P, OS, GT, WIDE], F32)
        scaled_bias = basis[:, 0, 0:GT, :]
        edge_ring = sb("edge_ring", [P, (GS + MS) * WIDE], F32)
        rows = edge_ring[:, 0:GS * WIDE].rearrange("p (s d) -> p s d", s=GS)
        msgs = edge_ring[:, GS * WIDE:(GS + MS) * WIDE].rearrange("p (s d) -> p s d", s=MS)
        mix = sb("mix", [P, 2, P], F32)
        index_now = sb("index_now", [P, U, 2], I32)
        act = sb("act", [P, 2, D], F32)
        actT = sb("actT", [P, 2, 2, D], F16)
        stats = sb("stats", [P, U, 6], F32)
        moments = sb("moments", [P, U, 2], F32)
        std = sb("std", [P, U], F32)
        rstd = sb("rstd", [P, U], F32)
        nmean = sb("nmean", [P, U], F32)
        eps = sb("eps", [P, 1], F32)
        same = sb("same", [P, ET, P], F16)
        rec = sb("rec", [P, 4, ET], F32)
        index = sb("index", [P, ET, 2], I32)
        tile_rel = sb("tile_rel", [P, ET], I32)
        dis = sb("dis", [P, NT], F32)
        ident = sb("ident", [P, P], F32)
        ones = sb("ones", [P, P], F32)
        before = sb("before", [P, P], F32)
        iota_i = sb("iota_i", [P, P], I32)
        iota = sb("iota", [P, P], F32)
        iota_nt = sb("iota_nt", [P, P], F32)
        spare_i = sb("spare_i", [P, 1], I32)
        spare = sb("spare", [P, 1], F32)
        zeros = sb("zeros", [P, WIDE], F32)
        edge_i = sb("edge_i", [P, 3, EC], I32)
        edge_w = sb("edge_w", [P, EC], F32)
        edge_f = sb("edge_f", [P, 3, EC], F32)
        counts = sb("counts", [P, 6, R], F32)
        counts_i = sb("counts_i", [P, R], I32)
        place = sb("place", [P, 5, EC], F32)
        place_i = sb("place_i", [P, 3, EC], I32)
        flag = sb("flag", [P, 3, ET], F32)

        psT = psum("psT", [P, 2, D])
        psZ = psum("psZ", [P, 2, D])
        psB = psum("psB", [P, 4, D])

        edges_in = sem("edges_in")
        consts_in = sem("consts_in")
        loops_in = [sem(f"loop_in{n}") for n in range(3)]
        basis_in = [sem(f"basis_in{n}") for n in range(2)]
        cleared = sem("cleared")
        pool_const = sem("pool_const")
        tables_zeroed = sem("tables_zeroed")
        graph_ready = sem("graph_ready")
        message_ends = sem("message_ends")
        ring_cleared = sem("ring_cleared")
        comp_scaled = sem("comp_scaled")
        dve_turn = sem("dve_turn")
        sp_turn = sem("sp_turn")
        setup = sem("setup")
        setup_pe = sem("setup_pe")
        picked = sem("picked")
        picked_used = sem("picked_used")
        spread = sem("spread")
        spread_pe = sem("spread_pe")
        same_done = sem("same_done")
        lower_done = sem("lower_done")
        counted = sem("counted")
        deg_hot = sem("deg_hot")
        deg_used = sem("deg_used")
        deg_std = sem("deg_std")
        split_hi = sem("split_hi")
        split_lo = sem("split_lo")
        combining = sem("combining")
        x_in = [sem(f"x_in{s}") for s in range(XS)]
        g_in = [sem(f"g_in{s}") for s in range(XS)]
        stored = [sem(f"stored{s}") for s in range(OS)]
        g_biased = sem("g_biased")
        bias_scaled = sem("bias_scaled")
        dis_put = sem("dis_put")
        gathered = [sem(f"gathered{s}") for s in range(GS)]
        index_put = sem("index_put")
        pool_turn = sem("pool_turn")
        added = sem("added")
        stat = sem("stat")
        moment = sem("moment")
        deviation = sem("deviation")
        inverse = sem("inverse")
        inverse_d = sem("inverse_d")
        shift = sem("shift")
        normed = sem("normed")
        mixed = sem("mixed")
        turned = sem("turned")
        hi_done = sem("hi_done")
        lo_done = sem("lo_done")
        product = sem("product")
        evac_v = sem("evac_v")
        evac_s = sem("evac_s")
        bias_row = sem("bias_row")
        rectified = sem("rectified")
        finished = sem("finished")

        by_node = "(p t) d -> p (t d)"
        x_nodes = x.rearrange(by_node, t=NT)
        out_nodes = out.rearrange(by_node, t=NT)
        acc1_nodes = acc1[0:N, :].rearrange(by_node, t=NT)
        acc2_nodes = acc2[0:N, :].rearrange(by_node, t=NT)
        acc3_nodes = acc3[0:N, :].rearrange(by_node, t=NT)
        PARTS = ((0, FULL), (FULL, NP))

        CH = 5
        CHUNKS = EC // CH
        jbytes, rbytes = CH * P, CH * 4 * ET
        hotJ = [edge_ring[0:EP, b * (jbytes + rbytes):b * (jbytes + rbytes) + jbytes]
                .rearrange("p (c j) -> p c j", c=CH) for b in range(2)]
        hotR = [edge_ring[0:EP, b * (jbytes + rbytes) + jbytes:(b + 1) * (jbytes + rbytes)]
                .rearrange("p (c f t) -> p c f t", c=CH, f=4) for b in range(2)]
        DQ = P
        dbytes = CH * DQ // 2 * 2 + CH * NT // 2
        hot16 = [edge_ring[0:EP, b * dbytes:(b + 1) * dbytes].bitcast(F16) for b in range(2)]
        reach = [h[:, 0:CH * DQ].rearrange("p (c q) -> p c q", c=CH) for h in hot16]
        hotQ = [h[:, CH * DQ:2 * CH * DQ].rearrange("p (c q) -> p c q", c=CH) for h in hot16]
        hotT = [h[:, 2 * CH * DQ:2 * CH * DQ + CH * NT].rearrange("p (c t) -> p c t", c=CH) for h in hot16]
        diag = [edge_ring[:, b * 4 * P:(b + 1) * 4 * P].rearrange("p (t j) -> p t j", t=4) for b in range(2)]
        low = [edge_ring[:, 8 * P + b * 2 * P:8 * P + (b + 1) * 2 * P].bitcast(F16)
               .rearrange("p (t j) -> p t j", t=4) for b in range(2)]
        mask = act[0:EP, 0, 0:R * EC]
        run = act[0:EP, 1, 0:R * EC]
        mask3 = mask.rearrange("p (r c) -> p r c", r=R)
        run3 = run.rearrange("p (r c) -> p r c", r=R)
        raw = [gring[:, 2 * n:2 * n + 2, :, :].rearrange("p s g d -> p (s g) d") for n in range(2)]

        block = ctx.enter_context(nc.Block())

        @block.sync
        def _(sp):
            for n, a in enumerate((src, dst, etype)):
                sp.dma_start(edge_i[0:EP, n, :], a.rearrange("(p c) -> p c", c=EC)).then_inc(edges_in, 16)
            sp.dma_start(edge_w[0:EP, :], weight.rearrange("(p c) -> p c", c=EC)).then_inc(edges_in, 16)
            for n, a in enumerate((loop0, loop1)):
                sp.dma_start(raw[n], a.rearrange("(c p) d -> p c d", p=P)).then_inc(loops_in[n], 16)
            for n, a in enumerate((comp0, comp1)):
                sp.dma_start(comp[n][:, :], a.rearrange("(o r) b -> o (r b)", o=1).to_broadcast([P, R * B]))\
                  .then_inc(consts_in, 16)
            for n, a in enumerate((bias0, bias1, bias2)):
                sp.dma_start(bias[n][:, :], a.rearrange("(o d) -> o d", o=1).to_broadcast([P, D]))\
                  .then_inc(consts_in, 16)
            for b in range(B):
                sp.dma_start(basis[:, b, :, :], basis0[b].rearrange("(c p) d -> p c d", p=P))\
                  .then_inc(basis_in[0], 16)
            sp.wait_ge(cleared, 1)
            sp.dma_start(acc1[N:N + P, :], zeros[:, 0:D]).then_inc(tables_zeroed, 16)
            sp.dma_start(acc2[N:N + P, :], zeros[:, :]).then_inc(tables_zeroed, 16)

            def load(ring, arrived, table, width, i, s):
                for a, b in PARTS:
                    source = table[a:b, bass.ds((i * XS + s) * (GT * width), GT * width)]
                    sp.dma_start(ring[a:b, s, :, 0:width], source.rearrange("p (g d) -> p g d", g=GT))\
                      .then_inc(arrived[s], 16)

            def store(table, width, i, s):
                for a, b in PARTS:
                    target = table[a:b, bass.ds((i * XS + s) * (GT * width), GT * width)]
                    sp.dma_start(target.rearrange("p (g d) -> p g d", g=GT), oring[a:b, s % OS, :, 0:width])\
                      .then_inc(stored[s % OS], 16)

            def hold(condition, value):
                sp.wait_ge(condition, value)
                if not isinstance(value, int):
                    sp.sem_inc(sp_turn, 1)

            def node_pass(load_group, release, store_group, done):
                last = NT // GT // XS - 1
                for s in range(XS):
                    load_group(0, s)

                def turn(i, s, more):
                    if more:
                        release(i * XS + s)
                        load_group(i + 1, s)
                    done(i * XS + s)
                    store_group(i, s)

                with sp.Fori(0, last) as i:
                    for s in range(XS):
                        turn(i, s, True)
                for s in range(XS):
                    turn(last, s, False)

            sp.wait_ge(ring_cleared, 1)
            node_pass(lambda i, s: load(xring, x_in, x_nodes, D, i, s),
                      lambda q: hold(normed, A.norm0 + GT * q + GT),
                      lambda i, s: store(acc1_nodes, D, i, s),
                      lambda q: hold(evac_v, A.evac0 + GT * q + GT))

            sp.wait_ge(combining, WB * R)
            for b in range(B):
                sp.dma_start(basis[:, b, :, :], basis1[b].rearrange("(c p) d -> p c d", p=P))\
                  .then_inc(basis_in[1], 16)
            sp.wait_ge(split_lo, 2)
            sp.dma_start(raw[0], w2t.rearrange("(c p) d -> p c d", p=P)).then_inc(loops_in[2], 16)
            acc3_rows = acc3[0:N, :].rearrange("(b p t) d -> b p t d", b=ZB, t=ZT)
            for b in range(ZB):
                sp.dma_start(acc3_rows[b], zeros[0:N // ZB // ZT, 0:D].unsqueeze(1)
                             .to_broadcast([N // ZB // ZT, ZT, D])).then_inc(tables_zeroed, 16)
            sp.dma_start(acc3[N:N + P, :], zeros[:, 0:D]).then_inc(tables_zeroed, 16)

            sp.wait_ge(split_lo, 3)
            sp.wait_ge(added, 16 * ET)

            def load_c(i, s):
                load(xring, x_in, acc1_nodes, D, i, s)
                load(gring, g_in, x_nodes, D, i, s)

            sp.wait_ge(cleared, 2)

            def done_c(q):
                hold(dis_put, q + 1)
                hold(evac_v, C.evac0 + GT * q + GT)

            def release_c(q):
                hold(turned, C.tile0 + GT * q + GT)
                hold(evac_v, C.evac0 + GT * q + GT)

            node_pass(load_c, release_c, lambda i, s: store(acc2_nodes, WIDE, i, s), done_c)

            sp.wait_ge(added, 16 * 3 * ET)

            def load_z(i, s):
                load(xring, x_in, acc2_nodes, WIDE, i, s)
                load(gring, g_in, acc3_nodes, D, i, s)

            def done_z(q):
                hold(finished, GT * q + GT)

            node_pass(load_z, done_z, lambda i, s: store(out_nodes, D, i, s), done_z)
            sp.wait_ge(tables_zeroed, 16 * (3 + ZB))
            for s in range(OS):
                sp.wait_ge(stored[s], 32 * (NT // GT // OS) * 3)

        @block.gpsimd
        def _(pool):
            pool.memset(zeros[:, :], 0.0).then_inc(cleared, 1)
            pool.memset(oring[:, :, :, D:WIDE], 0.0).then_inc(cleared, 1)
            pool.iota(iota_i[:, :], pattern=[[1, P]], base=0, channel_multiplier=0).then_inc(pool_const, 1)
            pool.iota(spare_i[:, :], pattern=[[1, 1]], base=N, channel_multiplier=1).then_inc(pool_const, 1)
            pool.memset(ones[:, :], 1.0).then_inc(pool_const, 1)
            pool.memset(ident[:, :], 0.0).then_inc(pool_const, 1)
            pool.wait_ge(pool_const, 4)
            pool.affine_select(out=ident[:, :], in_=ident[:, :], compare_op=ALU.not_equal, fill=1.0,
                               base=0, pattern=[[-1, P]], channel_multiplier=1).then_inc(pool_const, 1)
            pool.affine_select(out=before[:, :], in_=ones[:, :], compare_op=ALU.is_gt, fill=0.0,
                               base=0, pattern=[[1, P]], channel_multiplier=-1).then_inc(pool_const, 1)
            for n in range(ET // 4):
                pool.wait_ge(same_done, n + 1)
                wait(pool, counted, n - 1)
                pool.affine_select(out=low[n % 2], in_=same[:, 4 * n:4 * n + 4, :], compare_op=ALU.is_gt,
                                   fill=0.0, base=0, pattern=[[0, 4], [-1, P]], channel_multiplier=1)\
                    .then_inc(lower_done, 1)

            def hold(condition, value):
                pool.wait_ge(condition, value)
                if not isinstance(value, int):
                    pool.sem_inc(pool_turn, 1)

            def edge_pass(ep, table, width, sums, sum_width, ready):
                def step(i, k):
                    g = i * U + k + 5
                    if inside(g, ET):
                        s = (k + 5) % GS
                        pool.tensor_copy(index_now[:, (k + 5) % U, :], index[:, bass.ds(g, 1), :]
                                         .rearrange("p a b -> p (a b)")).then_inc(index_put, 1)
                        hold(index_put, ep.number * ET + g + 1)
                        if not isinstance(g, int) or g >= GS:
                            hold(normed, ep.norm0 + g - GS + 1)
                            hold(mixed, ep.number * ET + g - GS + 1)
                        pool.indirect_dma_start(
                            rows[:, s, 0:width], None, table,
                            bass.IndirectOffsetOnAxis(ap=index_now[:, (k + 5) % U, 0:1], axis=0))\
                            .then_inc(gathered[s], 16)
                    t = i * U + k
                    if inside(t, ET):
                        if ep is Fp:
                            hold(evac_v, ep.evac0 + t + 1)
                        else:
                            hold(evac_s, ep.evac0 + t + 1)
                        if isinstance(t, int) and t == 0:
                            ready()
                        else:
                            hold(added, 16 * (ep.number * ET + t))
                        pool.indirect_dma_start(
                            sums, bass.IndirectOffsetOnAxis(ap=index_now[:, k % U, 1:2], axis=0),
                            msgs[:, k % MS, 0:sum_width], None, compute_op=ALU.add).then_inc(added, 16)

                steps(pool, ET, U, 5, step)

            pool.wait_ge(graph_ready, 3)

            def ready_b():
                pool.wait_ge(tables_zeroed, 32)
                for s in range(OS):
                    pool.wait_ge(stored[s], 32 * (NT // GT // OS))

            edge_pass(Bp, x, D, acc1, D, ready_b)

            def step_c(i, k):
                if k % GT or k < 0:
                    return
                q = k // GT
                n = i * XS + q
                hold(g_in[q], 32 * (i + 1))
                pool.tensor_tensor(gring[:, q, :, :], gring[:, q, :, :],
                                   bias[1][:, :].unsqueeze(1).to_broadcast([P, GT, D]), ALU.add)\
                    .then_inc(g_biased, 1)
                hold(stored[q % OS], 32 * (NT // GT // OS + i * (XS // OS) + q // OS))
                pool.tensor_copy(oring[:, q % OS, :, D:D + 1], dis[:, bass.ds(n * GT, GT)].unsqueeze(2))\
                    .then_inc(dis_put, 1)

            steps(pool, NT, U, 0, step_c)

            def ready_d():
                pool.wait_ge(message_ends, 1)
                for s in range(OS):
                    pool.wait_ge(stored[s], 32 * 2 * (NT // GT // OS))

            pool.wait_ge(added, 16 * ET)
            edge_pass(Dp, acc1, D, acc2, WIDE, ready_d)

            pool.wait_ge(added, 16 * 2 * ET)
            edge_pass(Fp, acc2, WIDE, acc3, D, lambda: pool.wait_ge(tables_zeroed, 16 * (3 + ZB)))

            def step_z(i, k):
                if k < 0:
                    return
                q, j = k // GT, k % GT
                if j == 0:
                    hold(x_in[q], 32 * (2 * NT // GT // XS + i + 1))
                t = i * U + k
                if not isinstance(t, int) or t >= GT:
                    hold(g_biased, NT // GT + t - GT + 1)
                pool.tensor_scalar(scaled_bias[:, j, :], bias[2][:, :], xring[:, q, j, D:D + 1], None, ALU.mult)\
                    .then_inc(bias_scaled, 1)
                if j == 0:
                    hold(g_in[q], 32 * (NT // GT // XS + i + 1))
                hold(bias_scaled, t + 1)
                pool.tensor_tensor(gring[:, q, j, :], gring[:, q, j, :], scaled_bias[:, j, :], ALU.add)\
                    .then_inc(g_biased, 1)

            steps(pool, NT, U, 0, step_z)

        @block.scalar
        def _(sc):
            sc.wait_ge(loops_in[0], 16)
            sc.activation(node_w[0][:, 0, :, :], raw[0], ACT.Copy, scale=SCALE).then_inc(split_hi, 1)
            sc.wait_ge(loops_in[1], 16)
            sc.activation(node_w[1][:, 0, :, :], raw[1], ACT.Copy, scale=SCALE).then_inc(split_hi, 1)
            sc.wait_ge(deg_std, 1)
            sc.activation(dis[:, :], dis[:, :], ACT.Sqrt).then_inc(deg_std, 1)

            def std_unit(pp, n, col, width):
                per = width
                sc.wait_ge(moment, pp.ln0 + per * n + per)
                sc.activation(std[:, col:col + width], moments[:, col:col + width, 1], ACT.Sqrt,
                              bias=eps[:, 0:1]).then_inc(deviation, 1)

            def split_high(pp, t, k):
                sc.wait_ge(turned, pp.tile0 + t + 1)
                wait(sc, product, pp.tile0 + t - 1)
                sc.activation(actT[:, k % 2, 0, :], psT[:, k % 2, :], ACT.Relu if pp is C else ACT.Copy)\
                  .then_inc(hi_done, 1)

            def node_step(pp, i, k):
                if pp.ln0 is not None:
                    a = i * U + k + 2
                    if inside(a, NT):
                        c = (k + 2) % U
                        q, j = c // GT, c % GT
                        if j == 0:
                            unit = (i * U + k + 2) // GT if isinstance(i, int) else i * (U // GT) + (k + 2) // GT
                            sc.wait_ge(shift, pp.unit0 + unit + 1)
                        wait(sc, turned, pp.tile0 + a - 1)
                        sc.activation(act[:, c % 2, :], xring[:, q, j, 0:D], ACT.Relu,
                                      scale=rstd[:, c:c + 1], bias=nmean[:, c:c + 1]).then_inc(normed, 1)
                b = i * U + k + 1
                if inside(b, NT):
                    split_high(pp, b, k + 1)
                t = i * U + k
                if pp is Z and inside(t, NT):
                    c = k % U
                    q, j = c // GT, c % GT
                    sc.wait_ge(evac_v, pp.evac0 + t + 1)
                    sc.activation(oring[:, q % OS, j, 0:D], oring[:, q % OS, j, 0:D], ACT.Relu,
                                  scale=xring[:, q, j, D:D + 1]).then_inc(rectified, 1)
                if pp.ln0 is not None and k % GT == 1:
                    u = i * U + k + 3
                    if inside(u, NT):
                        unit = i * (U // GT) + (k + 3) // GT
                        std_unit(pp, unit, (k + 3) % U, GT)

            def edge_step(ep, i, k):
                a = i * U + k + 3
                if ep.ln0 is not None and inside(a, ET):
                    std_unit(ep, a, (k + 3) % U, 1)
                b = i * U + k + 2
                if inside(b, ET):
                    c = (k + 2) % U
                    s = c % GS
                    wait(sc, turned, ep.tile0 + b - 1)
                    if ep.ln0 is not None:
                        sc.wait_ge(shift, ep.unit0 + b + 1)
                        sc.activation(act[:, c % 2, :], rows[:, s, 0:D], ACT.Relu,
                                      scale=rstd[:, c:c + 1], bias=nmean[:, c:c + 1]).then_inc(normed, 1)
                    else:
                        sc.wait_ge(gathered[s], 16 * (ep.number * ET // GS + i * (U // GS) + (k + 2) // GS + 1))
                        sc.activation(act[:, c % 2, :], rows[:, s, 0:D], ACT.Relu).then_inc(normed, 1)
                h = i * U + k + 1
                if inside(h, ET):
                    split_high(ep, h, k + 1)
                t = i * U + k
                if ep is not Fp and inside(t, ET):
                    sc.wait_ge(product, ep.tile0 + t + 1)
                    wait(sc, added, 16 * (ep.number * ET + t - MS + 1))
                    sc.activation(msgs[:, k % MS, 0:D], psZ[:, k % 2, :], ACT.Copy, scale=1.0 / SCALE)\
                      .then_inc(evac_s, 1)

            steps(sc, NT, U, 4, lambda i, k: node_step(A, i, k))
            steps(sc, ET, U, 3, lambda i, k: edge_step(Bp, i, k))
            sc.wait_ge(loops_in[2], 16)
            sc.activation(node_w[0][:, 0, :, :], raw[0], ACT.Copy, scale=SCALE).then_inc(split_hi, 1)
            steps(sc, NT, U, 4, lambda i, k: node_step(C, i, k))
            steps(sc, ET, U, 3, lambda i, k: edge_step(Dp, i, k))
            steps(sc, ET, U, 3, lambda i, k: edge_step(Fp, i, k))
            steps(sc, NT, U, 4, lambda i, k: node_step(Z, i, k))

        @block.vector
        def _(v):
            done = [0]

            def link(ins):
                done[0] += 1
                ins.then_inc(setup, 1)
                v.wait_ge(setup, done[0])

            v.memset(xring[96:P, :, :, :], 0.0).then_inc(ring_cleared, 1)
            link(v.memset(eps[:, :], EPS))
            v.wait_ge(pool_const, 6)
            v.tensor_copy(iota[:, :], iota_i[:, :]).then_inc(setup, 1)
            done[0] += 1
            link(v.tensor_copy(spare[:, :], spare_i[:, :]))
            link(v.tensor_scalar(iota_nt[:, :], iota[:, :], float(NT), None, ALU.mult))

            def split_low(n, slot, weights):
                v.wait_ge(split_hi, n + 1)
                v.scalar_tensor_tensor(out=weights[:, 1, :, :].rearrange("p c d -> p (c d)"),
                                       in0=raw[slot].rearrange("p c d -> p (c d)"), scalar=SCALE,
                                       in1=weights[:, 0, :, :].rearrange("p c d -> p (c d)"),
                                       op0=ALU.mult, op1=ALU.subtract).then_inc(split_lo, 1)

            split_low(0, 0, node_w[0])
            split_low(1, 1, node_w[1])

            v.wait_ge(edges_in, 64)
            link(v.tensor_copy(edge_f[0:EP, :, :], edge_i[0:EP, :, :]))
            link(v.tensor_tensor(mask3, edge_f[0:EP, 2, :].unsqueeze(1).to_broadcast([EP, R, EC]),
                                 iota[0:EP, 0:R].unsqueeze(2).to_broadcast([EP, R, EC]), ALU.is_equal))
            link(v.tensor_tensor_scan(run, ones[0:EP, 0:1].to_broadcast([EP, R * EC]), mask, 0.0,
                                      ALU.mult, ALU.add))
            link(v.tensor_copy(counts[0:EP, 0, :], run3[:, :, EC - 1]))
            link(v.tensor_tensor(run3[:, 1:R, :], run3[:, 1:R, :],
                                 counts[0:EP, 0, 0:R - 1].unsqueeze(2).to_broadcast([EP, R - 1, EC]), ALU.subtract))
            link(v.tensor_copy(counts[0:EP, 1, :], run3[:, :, EC - 1]))
            counted_here = done[0]
            v.wait_ge(setup_pe, 1)
            link(v.tensor_scalar(counts_i[:, :], psB[:, 1, 0:R], float(P - 1), None, ALU.add))
            link(v.tensor_scalar(counts_i[:, :], counts_i[:, :], 7, None, ALU.arith_shift_right))
            link(v.tensor_copy(counts[:, 2, :], counts_i[:, :]))
            link(v.tensor_tensor_scan(counts[:, 3, :], ones[:, 0:R], counts[:, 2, :], 0.0, ALU.mult, ALU.add))
            link(v.tensor_tensor(counts[:, 4, :], counts[:, 3, :], counts[:, 2, :], ALU.subtract))
            link(v.scalar_tensor_tensor(out=counts[:, 5, :], in0=counts[:, 4, :], scalar=float(P),
                                        in1=psB[:, 0, 0:R], op0=ALU.mult, op1=ALU.add))
            link(v.tensor_tensor(run3, run3, counts[0:EP, 5, :].unsqueeze(2).to_broadcast([EP, R, EC]), ALU.add))
            link(v.tensor_tensor(mask3, mask3, run3, ALU.mult))
            link(v.tensor_reduce(place[0:EP, 0, :], mask3.rearrange("p r c -> p c r"), AX_X, ALU.add))
            link(v.tensor_scalar(place_i[0:EP, 0, :], place[0:EP, 0, :], -1.0, None, ALU.add))
            link(v.tensor_scalar(place_i[0:EP, 1, :], place_i[0:EP, 0, :], 7, None, ALU.arith_shift_right))
            link(v.tensor_scalar(place_i[0:EP, 2, :], place_i[0:EP, 0, :], P - 1, None, ALU.bitwise_and))
            link(v.tensor_copy(place[0:EP, 1:3, :], place_i[0:EP, 1:3, :]))

            last_rel = act[:, 0, 0:ET * R].rearrange("p (t r) -> p t r", t=ET)
            link(v.tensor_tensor(last_rel, counts[:, 3, :].unsqueeze(1).to_broadcast([P, ET, R]),
                                 iota[:, 0:ET].unsqueeze(2).to_broadcast([P, ET, R]), ALU.is_le))
            link(v.tensor_reduce(flag[:, 0, :], last_rel, AX_X, ALU.add))
            v.tensor_scalar(tile_rel[:, :], flag[:, 0, :], float(R - 1), None, ALU.min).then_inc(graph_ready, 1)

            for n in range(CHUNKS):
                c0 = n * CH
                wait(v, picked_used, n - 1)
                v.tensor_tensor(hotJ[n % 2], iota[0:EP, :].unsqueeze(1).to_broadcast([EP, CH, P]),
                                place[0:EP, 2, c0:c0 + CH].unsqueeze(2).to_broadcast([EP, CH, P]),
                                ALU.is_equal).then_inc(picked, 1)
                v.tensor_tensor(hotR[n % 2][:, :, 3, :], iota[0:EP, 0:ET].unsqueeze(1).to_broadcast([EP, CH, ET]),
                                place[0:EP, 1, c0:c0 + CH].unsqueeze(2).to_broadcast([EP, CH, ET]),
                                ALU.is_equal).then_inc(picked, 1)
                v.wait_ge(picked, 5 * n + 2)
                for f, a in enumerate((edge_f[0:EP, 0, :], edge_f[0:EP, 1, :], edge_w[0:EP, :])):
                    v.tensor_tensor(hotR[n % 2][:, :, f, :], hotR[n % 2][:, :, 3, :],
                                    a[:, c0:c0 + CH].unsqueeze(2).to_broadcast([EP, CH, ET]), ALU.mult)\
                     .then_inc(picked, 1)
            v.wait_ge(picked_used, CHUNKS)
            link(v.tensor_copy(rec[:, :, :].rearrange("p f t -> p (f t)"), psB[:, 2, 0:4 * ET]))
            link(v.tensor_scalar(flag[:, 0, :], rec[:, 3, :], -1.0, 1.0, ALU.mult, ALU.add))
            link(v.scalar_tensor_tensor(out=rec[:, 1, :], in0=flag[:, 0, :], scalar=spare[:, 0:1],
                                        in1=rec[:, 1, :], op0=ALU.mult, op1=ALU.add))
            def compare(n):
                v.wait_ge(spread_pe, n + 1)
                v.tensor_tensor(same[:, 4 * n:4 * n + 4, :],
                                psB[:, n % 2, :].rearrange("p (t j) -> p t j", t=4),
                                rec[:, 1, 4 * n:4 * n + 4].unsqueeze(2).to_broadcast([P, 4, P]),
                                ALU.is_equal).then_inc(same_done, 1)

            def count(n):
                v.wait_ge(lower_done, n + 1)
                v.tensor_reduce(flag[:, 1, 4 * n:4 * n + 4], low[n % 2], AX_X, ALU.add).then_inc(counted, 1)

            for n in range(ET // 4 + 2):
                if n < ET // 4:
                    wait(v, spread_pe, n - 1)
                    v.tensor_tensor(diag[n % 2], ident[:, :].unsqueeze(1).to_broadcast([P, 4, P]),
                                    rec[:, 1, 4 * n:4 * n + 4].unsqueeze(2).to_broadcast([P, 4, P]),
                                    ALU.mult).then_inc(spread, 1)
                if 1 <= n <= ET // 4:
                    compare(n - 1)
                if n >= 2:
                    count(n - 2)
            v.wait_ge(counted, ET // 4)
            link(v.tensor_scalar(flag[:, 1, :], flag[:, 1, :], 0.5, None, ALU.is_gt))
            link(v.tensor_scalar(flag[:, 2, :], rec[:, 1, :], spare[:, 0:1], None, ALU.subtract))
            link(v.tensor_tensor(flag[:, 2, :], flag[:, 2, :], flag[:, 1, :], ALU.mult))
            link(v.tensor_tensor(flag[:, 2, :], rec[:, 1, :], flag[:, 2, :], ALU.subtract))
            v.tensor_copy(index[:, :, 1], flag[:, 2, :]).then_inc(setup, 1)
            done[0] += 1
            v.tensor_copy(index[:, :, 0], rec[:, 0, :]).then_inc(graph_ready, 1)

            for n in range(CHUNKS):
                c0 = n * CH
                b = n % 2
                wait(v, deg_used, n - 1)
                v.tensor_tensor(reach[b], iota_nt[0:EP, :].unsqueeze(1).to_broadcast([EP, CH, P]),
                                edge_f[0:EP, 0, c0:c0 + CH].unsqueeze(2).to_broadcast([EP, CH, P]),
                                ALU.is_le).then_inc(deg_hot, 1)
                v.wait_ge(deg_hot, 7 * n + 1)
                v.tensor_reduce(place[0:EP, 3, c0:c0 + CH], reach[b], AX_X, ALU.add).then_inc(deg_hot, 1)
                v.wait_ge(deg_hot, 7 * n + 2)
                v.tensor_scalar(place[0:EP, 4, c0:c0 + CH], place[0:EP, 3, c0:c0 + CH], -float(NT), float(NT),
                                ALU.mult, ALU.add).then_inc(deg_hot, 1)
                v.wait_ge(deg_hot, 7 * n + 3)
                v.tensor_tensor(place[0:EP, 4, c0:c0 + CH], place[0:EP, 4, c0:c0 + CH],
                                edge_f[0:EP, 0, c0:c0 + CH], ALU.add).then_inc(deg_hot, 1)
                v.tensor_scalar(place[0:EP, 3, c0:c0 + CH], place[0:EP, 3, c0:c0 + CH], -1.0, None, ALU.add)\
                 .then_inc(deg_hot, 1)
                v.wait_ge(deg_hot, 7 * n + 5)
                v.tensor_tensor(hotT[b], iota[0:EP, 0:NT].unsqueeze(1).to_broadcast([EP, CH, NT]),
                                place[0:EP, 4, c0:c0 + CH].unsqueeze(2).to_broadcast([EP, CH, NT]),
                                ALU.is_equal).then_inc(deg_hot, 1)
                v.tensor_tensor(hotQ[b], iota[0:EP, :].unsqueeze(1).to_broadcast([EP, CH, P]),
                                place[0:EP, 3, c0:c0 + CH].unsqueeze(2).to_broadcast([EP, CH, P]),
                                ALU.is_equal).then_inc(deg_hot, 1)
            v.wait_ge(deg_used, CHUNKS)
            v.tensor_scalar(dis[:, :], psB[:, 1, 0:NT], 1.0, None, ALU.add).then_inc(deg_std, 1)
            v.wait_ge(deg_std, 2)
            v.reciprocal(dis[:, :], dis[:, :]).then_inc(graph_ready, 1)
            v.wait_ge(consts_in, 80)
            for n in range(2):
                v.tensor_scalar(comp[n][:, :], comp[n][:, :], SCALE, None, ALU.mult).then_inc(comp_scaled, 1)
            v.wait_ge(comp_scaled, 2)

            def combine(layer, i, kc):
                base = WB * R * layer + (i - 1) * WB + 6 * kc
                r = i - 1
                at = r * (2 * KC * D)
                hi = rel_w[:, bass.ds(at + kc * D, D)]
                lo = rel_w[:, bass.ds(at + (KC + kc) * D, D)]
                if kc == 0:
                    v.wait_ge(basis_in[layer], 16 * B)
                for b in range(B):
                    c = comp[layer][:, bass.ds(r * B + b, 1)]
                    if b == 0:
                        ins = v.tensor_scalar(combined[:, :], basis[:, b, kc, :], c, None, ALU.mult)
                    else:
                        v.wait_ge(combining, base + b)
                        ins = v.scalar_tensor_tensor(out=combined[:, :], in0=basis[:, b, kc, :], scalar=c,
                                                     in1=combined[:, :], op0=ALU.mult, op1=ALU.add)
                    ins.then_inc(combining, 1)
                v.wait_ge(combining, base + B)
                v.tensor_copy(hi, combined[:, :]).then_inc(combining, 1)
                v.wait_ge(combining, base + B + 1)
                v.tensor_tensor(lo, combined[:, :], hi, ALU.subtract).then_inc(combining, 1)
                v.wait_ge(combining, base + B + 2)

            def tile_stats(pp, t, c, rows_of):
                v.bn_stats(stats[:, c, :], rows_of).then_inc(stat, 1)
                v.wait_ge(stat, pp.ln0 + t + 1)
                if not isinstance(t, int):
                    v.sem_inc(dve_turn, 1)
                v.bn_aggr(moments[:, c, :], stats[:, c, :]).then_inc(moment, 1)

            def scale_and_shift(pp, unit, c, w, degrees=None):
                v.wait_ge(deviation, pp.unit0 + unit + 1)
                v.reciprocal(rstd[:, c:c + w], std[:, c:c + w]).then_inc(inverse, 1)
                v.wait_ge(inverse, pp.unit0 + unit + 1)
                if degrees is not None:
                    v.tensor_tensor(rstd[:, c:c + w], rstd[:, c:c + w], degrees, ALU.mult).then_inc(inverse_d, 1)
                    v.wait_ge(inverse_d, unit + 1)
                v.scalar_tensor_tensor(out=nmean[:, c:c + w], in0=moments[:, c:c + w, 0], scalar=-1.0,
                                       in1=rstd[:, c:c + w], op0=ALU.mult, op1=ALU.mult).then_inc(shift, 1)

            def split_lower(pp, t, k):
                v.wait_ge(hi_done, pp.tile0 + t + 1)
                s = k % 2
                if pp is C:
                    ins = v.scalar_tensor_tensor(out=actT[:, s, 1, :], in0=psT[:, s, :], scalar=0.0,
                                                 in1=actT[:, s, 0, :], op0=ALU.max, op1=ALU.subtract)
                else:
                    ins = v.tensor_tensor(actT[:, s, 1, :], psT[:, s, :], actT[:, s, 0, :], ALU.subtract)
                ins.then_inc(lo_done, 1)

            def node_step(pp, i, k):
                if pp.ln0 is not None:
                    a = i * U + k + 4
                    if inside(a, NT):
                        c = (k + 4) % U
                        q, j = c // GT, c % GT
                        if j == 0:
                            v.wait_ge(x_in[q], 32 * (pp.number * (NT // GT // XS) + i + (k + 4) // U + 1))
                        tile_stats(pp, a, c, xring[:, q, j, 0:D])
                    u = i * U + k + 2
                    if k % GT == 0 and inside(u, NT):
                        c = (k + 2) % U
                        q = c // GT
                        scale_and_shift(pp, i * (U // GT) + (k + 2) // GT, c, GT,
                                        xring[:, q, :, D:D + 1].rearrange("p g o -> p (g o)") if pp is Z else None)
                b = i * U + k + 1
                if inside(b, NT):
                    split_lower(pp, b, k + 1)
                t = i * U + k
                if pp is Z and inside(t - 1, NT):
                    finish(i, k - 1)
                if inside(t, NT):
                    c = k % U
                    q, j = c // GT, c % GT
                    if j == 0:
                        wait(v, stored[q % OS], 32 * (pp.number * (NT // GT // OS) + i * (XS // OS) + q // OS))
                    v.wait_ge(product, pp.tile0 + t + 1)
                    if pp is A:
                        other = bias[0][:, :]
                    elif pp is C:
                        other = gring[:, q, j, :]
                        v.wait_ge(g_biased, i * (U // GT) + q + 1)
                    else:
                        other = gring[:, q, j, :]
                        v.wait_ge(g_biased, NT // GT + t + 1)
                    v.scalar_tensor_tensor(out=oring[:, q % OS, j, 0:D], in0=psZ[:, k % 2, :], scalar=1.0 / SCALE,
                                           in1=other, op0=ALU.mult, op1=ALU.add).then_inc(evac_v, 1)
                if pp is not Z and not isinstance(i, int) and k % 2 == 1:
                    combine(pp.number, i, k // 2)

            def finish(i, k):
                t = i * U + k
                c = k % U
                q, j = c // GT, c % GT
                v.wait_ge(rectified, t + 1)
                o = oring[:, q % OS, j, 0:D]
                v.tensor_tensor(o, o, xring[:, q, j, 0:D], ALU.add).then_inc(finished, 1)

            def edge_step(ep, i, k):
                a = i * U + k + 3
                if ep.ln0 is not None and inside(a, ET):
                    c = (k + 3) % U
                    s = c % GS
                    v.wait_ge(gathered[s], 16 * (ep.number * ET // GS + i * (U // GS) + (k + 3) // GS + 1))
                    tile_stats(ep, a, c, rows[:, s, 0:D])
                b = i * U + k + 2
                if inside(b, ET):
                    c = (k + 2) % U
                    s = c % GS
                    if ep.ln0 is not None:
                        scale_and_shift(ep, b, c, 1)
                    wait(v, turned, ep.tile0 + b - 1)
                    if ep is Fp:
                        v.tensor_scalar(mix[:, c % 2, :], same[:, bass.ds(b, 1), :].rearrange("p a j -> p (a j)"),
                                        rows[:, s, D:D + 1], rec[:, 3, bass.ds(b, 1)], ALU.mult, ALU.mult)\
                         .then_inc(mixed, 1)
                    else:
                        v.tensor_scalar(mix[:, c % 2, :], same[:, bass.ds(b, 1), :].rearrange("p a j -> p (a j)"),
                                        rec[:, 2, bass.ds(b, 1)], None, ALU.mult).then_inc(mixed, 1)
                h = i * U + k + 1
                if inside(h, ET):
                    split_lower(ep, h, k + 1)
                t = i * U + k
                if ep is Fp and inside(t, ET):
                    v.wait_ge(product, ep.tile0 + t + 1)
                    v.wait_ge(evac_v, ep.evac0 + t - 1)
                    v.tensor_scalar(bias_rows[:, k % 2, :], bias[2][:, :], psB[:, k % 4, 0:1], None, ALU.mult)\
                     .then_inc(bias_row, 1)
                    wait(v, added, 16 * (ep.number * ET + t - MS + 1))
                    v.wait_ge(bias_row, t + 1)
                    v.scalar_tensor_tensor(out=msgs[:, k % MS, 0:D], in0=psZ[:, k % 2, :], scalar=1.0 / SCALE,
                                           in1=bias_rows[:, k % 2, :], op0=ALU.mult, op1=ALU.add).then_inc(evac_v, 1)

            steps(v, NT, U, 4, lambda i, k: node_step(A, i, k))
            v.memset(msgs[:, :, D:WIDE], 0.0).then_inc(message_ends, 1)
            steps(v, ET, U, 3, lambda i, k: edge_step(Bp, i, k))
            split_low(2, 0, node_w[0])
            steps(v, NT, U, 4, lambda i, k: node_step(C, i, k))
            steps(v, ET, U, 3, lambda i, k: edge_step(Dp, i, k))
            steps(v, ET, U, 3, lambda i, k: edge_step(Fp, i, k))
            steps(v, NT, U, 4, lambda i, k: node_step(Z, i, k))
            finish(NT // U - 1, U - 1)

        @block.tensor
        def _(pe):
            pe.wait_ge(setup, 10)
            pe.wait_ge(pool_const, 6)
            pe.matmul(psB[:, 0, 0:R], before[0:EP, :], counts[0:EP, 1, :], start=True, stop=True)
            pe.matmul(psB[:, 1, 0:R], ones[0:EP, :], counts[0:EP, 1, :], start=True, stop=True)\
              .then_inc(setup_pe, 1)
            for n in range(CHUNKS):
                pe.wait_ge(picked, 5 * n + 5)
                for c in range(CH):
                    last = pe.matmul(psB[:, 2, 0:4 * ET], hotJ[n % 2][:, c, :],
                                     hotR[n % 2][:, c, :, :].rearrange("p f t -> p (f t)"),
                                     start=(n == 0 and c == 0), stop=(n == CHUNKS - 1 and c == CH - 1))
                last.then_inc(picked_used, 1)
            for n in range(ET // 4):
                pe.wait_ge(spread, n + 1)
                wait(pe, same_done, n - 1)
                pe.matmul(psB[:, n % 2, :], ones[:, :], diag[n % 2].rearrange("p t j -> p (t j)"),
                          start=True, stop=True).then_inc(spread_pe, 1)
            pe.wait_ge(same_done, ET // 4)
            for n in range(CHUNKS):
                pe.wait_ge(deg_hot, 7 * n + 7)
                for c in range(CH):
                    last = pe.matmul(psB[:, 1, 0:NT], hotQ[n % 2][:, c, :], hotT[n % 2][:, c, :],
                                     start=(n == 0 and c == 0), stop=(n == CHUNKS - 1 and c == CH - 1))
                last.then_inc(deg_used, 1)

            def multiply(pp, t, k, weights):
                pe.wait_ge(lo_done, pp.tile0 + t + 1)
                s = k % 2
                for c in range(KC):
                    for part, half in ((0, 0), (0, 1), (1, 0)):
                        last = pe.matmul(psZ[:, s, :], actT[:, s, part, c * P:(c + 1) * P], weights(half, c),
                                         start=(c == 0 and part == 0 and half == 0), stop=(c == KC - 1 and part == 1))
                last.then_inc(product, 1)

            def turn_slot_free(pp, t):
                wait(pe, lo_done, pp.tile0 + t - 1)

            def node_step(pp, i, k, w):
                a = i * U + k + 1
                if inside(a, NT):
                    c = (k + 1) % U
                    q, j = c // GT, c % GT
                    if pp is C:
                        if j == 0:
                            pe.wait_ge(x_in[q], 32 * (pp.number * (NT // GT // XS) + i + (k + 1) // U + 1))
                        source = xring[:, q, j, 0:D]
                    else:
                        pe.wait_ge(normed, pp.norm0 + a + 1)
                        source = act[:, c % 2, :]
                    turn_slot_free(pp, a)
                    for n in range(KC):
                        last = pe.transpose(psT[:, c % 2, n * P:(n + 1) * P], source[:, n * P:(n + 1) * P], ident[:, :])
                    last.then_inc(turned, 1)
                t = i * U + k
                if inside(t, NT):
                    if isinstance(t, int) and t < 2:
                        if pp is C:
                            pe.wait_ge(evac_s, Bp.evac0 + ET - 1 + t)
                        elif pp is Z:
                            pe.wait_ge(evac_v, pp.evac0 - 1 + t)
                    else:
                        pe.wait_ge(evac_v, pp.evac0 + t - 1)
                    multiply(pp, t, k, lambda half, c: w[:, half, c, :])

            def edge_step(ep, i, k):
                a = i * U + k + 1
                if inside(a, ET):
                    c = (k + 1) % U
                    pe.wait_ge(normed, ep.norm0 + a + 1)
                    pe.wait_ge(mixed, ep.number * ET + a + 1)
                    turn_slot_free(ep, a)
                    for n in range(KC):
                        last = pe.matmul(psT[:, c % 2, n * P:(n + 1) * P], act[:, c % 2, n * P:(n + 1) * P],
                                         mix[:, c % 2, :], start=True, stop=True)
                    if ep is Fp:
                        if not isinstance(a, int) or a >= 4:
                            pe.wait_ge(evac_v, ep.evac0 + a - 3)
                        last = pe.matmul(psB[:, c % 4, 0:1], mix[:, c % 2, :], ones[:, 0:1],
                                         start=True, stop=True)
                    last.then_inc(turned, 1)
                t = i * U + k
                if inside(t, ET):
                    if ep is Fp:
                        weights = lambda half, c: node_w[0][:, half, c, :]
                    else:
                        r = pe.value_load(tile_rel[0:1, bass.ds(t, 1)], min_val=0, max_val=R - 1)
                        weights = lambda half, c: rel_w[:, bass.ds(r * (2 * KC * D) + (half * KC + c) * D, D)]
                    if isinstance(t, int) and t < 2:
                        if ep is Fp:
                            pe.wait_ge(evac_s, Dp.evac0 + ET - 1 + t)
                        elif ep is Dp:
                            pe.wait_ge(evac_v, C.evac0 + NT - 1 + t)
                        else:
                            pe.wait_ge(evac_v, A.evac0 + NT - 1 + t)
                    elif ep is Fp:
                        pe.wait_ge(evac_v, ep.evac0 + t - 1)
                    else:
                        pe.wait_ge(evac_s, ep.evac0 + t - 1)
                    multiply(ep, t, k, weights)

            pe.wait_ge(split_lo, 1)
            steps(pe, NT, U, 1, lambda i, k: node_step(A, i, k, node_w[0]))
            pe.wait_ge(combining, WB * R)
            pe.wait_ge(graph_ready, 1)
            steps(pe, ET, U, 1, lambda i, k: edge_step(Bp, i, k))
            pe.wait_ge(split_lo, 2)
            steps(pe, NT, U, 1, lambda i, k: node_step(C, i, k, node_w[1]))
            pe.wait_ge(combining, 2 * WB * R)
            steps(pe, ET, U, 1, lambda i, k: edge_step(Dp, i, k))
            pe.wait_ge(split_lo, 3)
            steps(pe, ET, U, 1, lambda i, k: edge_step(Fp, i, k))
            steps(pe, NT, U, 1, lambda i, k: node_step(Z, i, k, node_w[0]))


def kernel(x, src, dst, edge_type_8, edge_weight, L0_gnn_basis0, L0_gnn_comp0, L0_gnn_bias0, L0_gnn_loop0,
           L0_gnn_basis1, L0_gnn_comp1, L0_gnn_bias1, L0_gnn_loop1, L1_gnn_W, L1_gnn_b):
    import numpy as np
    import concourse.bacc as bacc
    from concourse.bass_utils import run_bass_kernel_spmd

    nc = bacc.Bacc("TRN2", target_bir_lowering=False, num_devices=1)
    inputs = [("x", x), ("src", src), ("dst", dst), ("etype", edge_type_8), ("weight", edge_weight),
              ("basis0", L0_gnn_basis0), ("comp0", L0_gnn_comp0), ("bias0", L0_gnn_bias0), ("loop0", L0_gnn_loop0),
              ("basis1", L0_gnn_basis1), ("comp1", L0_gnn_comp1), ("bias1", L0_gnn_bias1), ("loop1", L0_gnn_loop1),
              ("w2t", np.asarray(L1_gnn_W).T), ("bias2", L1_gnn_b)]
    arrays, args = {}, []
    for name, a in inputs:
        a = np.ascontiguousarray(a)
        arrays[f"in_{name}"] = a
        args.append(nc.dram_tensor(f"in_{name}", a.shape, mybir.dt.from_np(a.dtype), kind="ExternalInput").ap())
    out = nc.dram_tensor("out_x", tuple(x.shape), F32, kind="ExternalOutput").ap()
    gnn_kernel(nc, *args, out)
    r = run_bass_kernel_spmd(nc, [arrays], core_ids=[0])
    return r.results[0]["out_x"]
```

```python
from contextlib import ExitStack

import concourse.bass as bass
from concourse import mybir

P = 128
ALU = mybir.AluOpType
ACT = mybir.ActivationFunctionType
F32 = mybir.dt.float32
F16 = mybir.dt.float16
I32 = mybir.dt.int32
AX_X = mybir.AxisListType.X
EPS = 1e-5
SCALE = 64.0


def wait(eng, sem, value):
    if not isinstance(value, int) or value > 0:
        eng.wait_ge(sem, value)


def inside(t, count):
    return not isinstance(t, int) or 0 <= t < count


def steps(eng, tiles, unroll, lead, step, tail=0):
    for k in range(-lead, unroll):
        step(0, k)
    with eng.Fori(1, tiles // unroll - 1) as i:
        for k in range(unroll):
            step(i, k)
    for k in range(unroll + tail):
        step(tiles // unroll - 1, k)


class NodePass:

    def __init__(self, number, tile0, evac0, norm0=None, ln0=None, unit0=None, unroll=8, ahead=4):
        self.number, self.tile0, self.evac0 = number, tile0, evac0
        self.norm0, self.ln0, self.unit0, self.unroll = norm0, ln0, unit0, unroll
        self.ahead = ahead

    def set_rings(self, x, x_in, x_before, other, other_in, results, stored, stores_before):
        self.x, self.x_in, self.x_before = x, x_in, x_before
        self.other, self.other_in = other, other_in
        self.results, self.stored, self.stores_before = results, stored, stores_before


class EdgePass:

    def __init__(self, number, tile0, evac0, norm0, ln0=None, unit0=None):
        self.number, self.tile0, self.evac0 = number, tile0, evac0
        self.norm0, self.ln0, self.unit0 = norm0, ln0, unit0


def gnn_kernel(nc, x, src, dst, etype, weight, basis0, comp0, bias0, loop0,
               basis1, comp1, bias1, loop1, w2t, bias2, out):
    N, D = x.shape
    E = src.shape[0]
    R, B = comp0.shape
    KC = D // P
    NT = 80
    NP = N // NT
    GT = 2
    U = 8
    XS, OS = 4, 2
    EC = 40
    EP = E // EC
    ET = -(-((E + R * (P - 1)) // P) // U) * U
    GS, MS = 4, 4
    WIDE = D + 4
    ROWS = N + P
    FULL = NP // 16 * 16
    BLOCKS = R * KC
    ZS = 4
    assert NP * NT == N and EP * EC == E and NP <= P and EP <= P and ET == 48 and R == NT // U - 2 and B == 4

    acc1 = nc.dram_tensor("acc1", (ROWS, D), F32, kind="Internal").ap()
    acc2 = nc.dram_tensor("acc2", (ROWS, WIDE), F32, kind="Internal").ap()
    acc3 = nc.dram_tensor("acc3", (ROWS, D), F32, kind="Internal").ap()

    A = NodePass(0, 0, 0, norm0=0, ln0=0, unit0=0)
    Bp = EdgePass(0, NT, 0, norm0=NT, ln0=NT, unit0=NT // GT)
    C = NodePass(1, NT + ET, NT)
    Dp = EdgePass(1, 2 * NT + ET, ET, norm0=NT + ET)
    Fp = EdgePass(2, 2 * NT + 2 * ET, 2 * NT, norm0=NT + 2 * ET, ln0=NT + ET, unit0=NT // GT + ET)
    Z = NodePass(2, 2 * NT + 3 * ET, 2 * NT + ET, norm0=NT + 3 * ET, ln0=NT + 2 * ET, unit0=NT // GT + 2 * ET,
                 unroll=2 * U, ahead=6)

    with ExitStack() as ctx:
        def sb(name, shape, dt):
            return ctx.enter_context(nc.sbuf_tensor(name, shape, dt))

        def psum(name, shape):
            return ctx.enter_context(nc.psum_tensor(name, shape, F32))

        def sem(name):
            return ctx.enter_context(nc.semaphore(name))

        rel_w = sb("rel_w", [P, R * 2 * KC * D], F16)
        node_w = [sb(f"node_w{n}", [P, 2, KC, D], F16) for n in range(2)]
        basis = sb("basis", [P, B, KC, D], F32)
        combined = sb("combined", [P, 2, D], F32)
        comp = [sb(f"comp{n}", [P, R * B], F32) for n in range(2)]
        bias = [sb(f"bias{n}", [P, D], F32) for n in range(3)]
        bias_rows = basis[:, 1, 0:2, :]
        xring = sb("xring", [P, XS, GT, WIDE], F32)
        gring = sb("gring", [P, XS, GT, D], F32)
        oring = sb("oring", [P, OS, GT, WIDE], F32)
        scaled_bias = basis[:, 0, :, :]
        edge_ring = sb("edge_ring", [P, (GS + MS) * WIDE], F32)
        rows = edge_ring[:, 0:GS * WIDE].rearrange("p (s d) -> p s d", s=GS)
        msgs = edge_ring[:, GS * WIDE:(GS + MS) * WIDE].rearrange("p (s d) -> p s d", s=MS)
        mix = sb("mix", [P, 2, P], F32)
        index_now = sb("index_now", [P, U, 2], I32)
        act = sb("act", [P, 2, D], F32)
        actT = sb("actT", [P, 2, 2, D], F16)
        stats = sb("stats", [P, U, 6], F32)
        moments = sb("moments", [P, U, 2], F32)
        std = sb("std", [P, U], F32)
        rstd = sb("rstd", [P, U], F32)
        nmean = sb("nmean", [P, U], F32)
        eps = sb("eps", [P, 1], F32)
        same = sb("same", [P, ET, P], F16)
        rec = sb("rec", [P, 4, ET], F32)
        index = sb("index", [P, ET, 2], I32)
        tile_rel = sb("tile_rel", [P, ET], I32)
        dis = sb("dis", [P, NT], F32)
        ident = sb("ident", [P, P], F32)
        ones = sb("ones", [P, P], F32)
        before = oring[:, 1, 1, 0:P]
        iota_i = oring[:, 1, 1, P:2 * P].bitcast(I32)
        iota = sb("iota", [P, P], F32)
        iota_nt = sb("iota_nt", [P, P], F32)
        spare_i = sb("spare_i", [P, 1], I32)
        spare = sb("spare", [P, 1], F32)
        zeros = sb("zeros", [P, WIDE], F32)
        edge_i = oring[:, 0, 0, 0:3 * EC].bitcast(I32).rearrange("p (n c) -> p n c", n=3)
        edge_w = sb("edge_w", [P, EC], F32)
        edge_f = sb("edge_f", [P, 3, EC], F32)
        counts = sb("counts", [P, 6, R], F32)
        counts_i = sb("counts_i", [P, R], I32)
        place = oring[:, 1, 0, 0:5 * EC].rearrange("p (n c) -> p n c", n=5)
        place_i = oring[:, 0, 1, 0:3 * EC].bitcast(I32).rearrange("p (n c) -> p n c", n=3)
        flag = sb("flag", [P, 3, ET], F32)

        xs = [xring[:, s, :, :] for s in range(XS)]
        gs = [gring[:, s, :, :] for s in range(XS)]
        outs = [oring[:, s, :, :] for s in range(OS)]
        taken = [0]

        def over_rel_w(slots, width):
            found = []
            for _ in range(slots):
                a = taken[0]
                taken[0] = a + 2 * GT * width
                found.append(rel_w[:, a:a + 2 * GT * width].bitcast(F32).rearrange("p (g d) -> p g d", g=GT))
            return found

        z_xs = xs + over_rel_w(XS, WIDE)
        z_gs = gs + over_rel_w(XS, D)
        z_outs = outs + over_rel_w(OS, D)
        over_w = rel_w[96:P, 0:taken[0]].bitcast(F32)
        piece = taken[0] // 2 // U
        over_w = [over_w[:, n * piece:(n + 1) * piece] for n in range(U)]
        assert taken[0] <= R * 2 * KC * D and taken[0] % (2 * U) == 0

        psT = psum("psT", [P, 2, D])
        psZ = psum("psZ", [P, ZS, D])
        psB = psZ
        psS = psum("psS", [P, 2, D])

        edges_in = sem("edges_in")
        consts_in = sem("consts_in")
        loops_in = [sem(f"loop_in{n}") for n in range(3)]
        basis_in = [sem(f"basis_in{n}") for n in range(2)]
        cleared = sem("cleared")
        pool_const = sem("pool_const")
        tables_zeroed = sem("tables_zeroed")
        graph_ready = sem("graph_ready")
        message_ends = sem("message_ends")
        ring_cleared = sem("ring_cleared")
        comp_scaled = sem("comp_scaled")
        act_turn = sem("act_turn")
        dve_turn = sem("dve_turn")
        sp_turn = sem("sp_turn")
        setup = sem("setup")
        setup_pe = sem("setup_pe")
        picked = sem("picked")
        picked_used = sem("picked_used")
        spread = sem("spread")
        spread_pe = sem("spread_pe")
        same_done = sem("same_done")
        lower_done = sem("lower_done")
        counted = sem("counted")
        deg_hot = sem("deg_hot")
        deg_used = sem("deg_used")
        deg_std = sem("deg_std")
        split_hi = sem("split_hi")
        split_lo = sem("split_lo")
        bases_scaled = sem("bases_scaled")
        bases_added = sem("bases_added")
        rel_summed = sem("rel_summed")
        rel_high = sem("rel_high")
        rel_free = sem("rel_free")
        x_in = [sem(f"x_in{s}") for s in range(XS)]
        g_in = [sem(f"g_in{s}") for s in range(XS)]
        stored = [sem(f"stored{s}") for s in range(OS)]
        z_in = [sem(f"z_in{s}") for s in range(2 * XS)]
        z_other_in = [sem(f"z_other_in{s}") for s in range(2 * XS)]
        z_stored = [sem(f"z_stored{s}") for s in range(2 * OS)]
        g_biased = sem("g_biased")
        bias_scaled = sem("bias_scaled")
        dis_put = sem("dis_put")
        gathered = [sem(f"gathered{s}") for s in range(GS)]
        index_put = sem("index_put")
        pool_turn = sem("pool_turn")
        added = sem("added")
        stat = sem("stat")
        moment = sem("moment")
        deviation = sem("deviation")
        inverse = sem("inverse")
        inverse_d = sem("inverse_d")
        shift = sem("shift")
        normed = sem("normed")
        mixed = sem("mixed")
        turned = sem("turned")
        hi_done = sem("hi_done")
        lo_done = sem("lo_done")
        product = sem("product")
        evac_v = sem("evac_v")
        evac_s = sem("evac_s")
        bias_row = sem("bias_row")
        rectified = sem("rectified")
        finished = sem("finished")

        A.set_rings(xs, x_in, 0, None, None, outs, stored, 0)
        C.set_rings(xs, x_in, NT // GT // XS, gs, g_in, outs, stored, NT // GT // OS)
        Z.set_rings(z_xs, z_in, 0, z_gs, z_other_in, z_outs, z_stored, 0)

        by_node = "(p t) d -> p (t d)"
        x_nodes = x.rearrange(by_node, t=NT)
        out_nodes = out.rearrange(by_node, t=NT)
        acc1_nodes = acc1[0:N, :].rearrange(by_node, t=NT)
        acc2_nodes = acc2[0:N, :].rearrange(by_node, t=NT)
        acc3_nodes = acc3[0:N, :].rearrange(by_node, t=NT)
        PARTS = ((0, FULL), (FULL, NP))

        CH = 5
        CHUNKS = EC // CH
        jbytes, rbytes = CH * P, CH * 4 * ET
        hotJ = [edge_ring[0:EP, b * (jbytes + rbytes):b * (jbytes + rbytes) + jbytes]
                .rearrange("p (c j) -> p c j", c=CH) for b in range(2)]
        hotR = [edge_ring[0:EP, b * (jbytes + rbytes) + jbytes:(b + 1) * (jbytes + rbytes)]
                .rearrange("p (c f t) -> p c f t", c=CH, f=4) for b in range(2)]
        DQ = P
        dbytes = CH * DQ // 2 * 2 + CH * NT // 2
        hot16 = [edge_ring[0:EP, b * dbytes:(b + 1) * dbytes].bitcast(F16) for b in range(2)]
        reach = [h[:, 0:CH * DQ].rearrange("p (c q) -> p c q", c=CH) for h in hot16]
        hotQ = [h[:, CH * DQ:2 * CH * DQ].rearrange("p (c q) -> p c q", c=CH) for h in hot16]
        hotT = [h[:, 2 * CH * DQ:2 * CH * DQ + CH * NT].rearrange("p (c t) -> p c t", c=CH) for h in hot16]
        diag = [edge_ring[:, b * 4 * P:(b + 1) * 4 * P].rearrange("p (t j) -> p t j", t=4) for b in range(2)]
        low = [edge_ring[:, 8 * P + b * 2 * P:8 * P + (b + 1) * 2 * P].bitcast(F16)
               .rearrange("p (t j) -> p t j", t=4) for b in range(2)]
        mask = act[0:EP, 0, 0:R * EC]
        run = act[0:EP, 1, 0:R * EC]
        mask3 = mask.rearrange("p (r c) -> p r c", r=R)
        run3 = run.rearrange("p (r c) -> p r c", r=R)
        term = [[msgs[:, 2 * b + h, 0:D] for h in range(2)] for b in range(2)]
        raw = [gring[:, 2 * n:2 * n + 2, :, :].rearrange("p s g d -> p (s g) d") for n in range(2)]

        scale_at = ({0: 0, 2: 1, 4: 2, 6: 3}, {0: 0, 1: 1, 3: 2, 5: 3})
        sum_at = ({1: 0, 3: 1, 5: 2, 7: 3}, {1: 0, 2: 1, 4: 2, 6: 3})
        round_at = ({1: 0, 3: 1, 5: 2, 7: 3}, {2: 0, 3: 1, 5: 2, 7: 3})
        low_at = ({1: 0, 3: 1, 5: 2, 7: 3}, {2: 0, 4: 1, 6: 2, 7: 3})

        block = ctx.enter_context(nc.Block())

        @block.sync
        def _(sp):
            for n, a in enumerate((src, dst, etype)):
                sp.dma_start(edge_i[0:EP, n, :], a.rearrange("(p c) -> p c", c=EC)).then_inc(edges_in, 16)
            sp.dma_start(edge_w[0:EP, :], weight.rearrange("(p c) -> p c", c=EC)).then_inc(edges_in, 16)
            for n, a in enumerate((loop0, loop1)):
                sp.dma_start(raw[n], a.rearrange("(c p) d -> p c d", p=P)).then_inc(loops_in[n], 16)
            for n, a in enumerate((comp0, comp1)):
                sp.dma_start(comp[n][:, :], a.rearrange("(o r) b -> o (r b)", o=1).to_broadcast([P, R * B]))\
                  .then_inc(consts_in, 16)
            for n, a in enumerate((bias0, bias1, bias2)):
                sp.dma_start(bias[n][:, :], a.rearrange("(o d) -> o d", o=1).to_broadcast([P, D]))\
                  .then_inc(consts_in, 16)
            for b in range(B):
                sp.dma_start(basis[:, b, :, :], basis0[b].rearrange("(c p) d -> p c d", p=P))\
                  .then_inc(basis_in[0], 16)
            sp.wait_ge(cleared, 1)
            sp.dma_start(acc1[N:N + P, :], zeros[:, 0:D]).then_inc(tables_zeroed, 16)
            sp.dma_start(acc2[N:N + P, :], zeros[:, :]).then_inc(tables_zeroed, 16)

            def load(ring, arrived, table, width, i, s):
                for a, b in PARTS:
                    source = table[a:b, bass.ds((i * len(ring) + s) * (GT * width), GT * width)]
                    sp.dma_start(ring[s][a:b, :, 0:width], source.rearrange("p (g d) -> p g d", g=GT))\
                      .then_inc(arrived[s], 16)

            def store(pp, table, width, i, s):
                n = s % len(pp.results)
                for a, b in PARTS:
                    target = table[a:b, bass.ds((i * len(pp.x) + s) * (GT * width), GT * width)]
                    sp.dma_start(target.rearrange("p (g d) -> p g d", g=GT), pp.results[n][a:b, :, 0:width])\
                      .then_inc(pp.stored[n], 16)

            def hold(condition, value):
                sp.wait_ge(condition, value)
                if not isinstance(value, int):
                    sp.sem_inc(sp_turn, 1)

            def node_pass(pp, load_group, release, store_group, done):
                slots = len(pp.x)
                last = NT // GT // slots - 1

                def turn(i, s, more):
                    if more:
                        release(i * slots + s)
                        load_group(i + 1, s)
                    done(i * slots + s)
                    store_group(i, s)

                with sp.Fori(0, last) as i:
                    for s in range(slots):
                        turn(i, s, True)
                for s in range(slots):
                    turn(last, s, False)

            def store_a(i, s):
                store(A, acc1_nodes, D, i, s)
                for a, b in PARTS:
                    target = acc3_nodes[a:b, bass.ds((i * XS + s) * (GT * D), GT * D)]
                    sp.dma_start(target.rearrange("p (g d) -> p g d", g=GT),
                                 zeros[a:b, 0:D].unsqueeze(1).to_broadcast([b - a, GT, D])).then_inc(tables_zeroed, 16)

            def load_a(i, s):
                load(A.x, A.x_in, x_nodes, D, i, s)

            sp.dma_start(acc3[N:N + P, :], zeros[:, 0:D]).then_inc(tables_zeroed, 16)
            sp.wait_ge(ring_cleared, 1)
            for s in range(XS):
                load_a(0, s)
            node_pass(A, load_a,
                      lambda q: hold(normed, A.norm0 + GT * q + GT),
                      store_a,
                      lambda q: hold(evac_v, A.evac0 + GT * q + GT))
            sp.wait_ge(split_lo, 2)
            sp.dma_start(raw[0], w2t.rearrange("(c p) d -> p c d", p=P)).then_inc(loops_in[2], 16)

            sp.wait_ge(rel_free, BLOCKS + 2)
            with sp.Fori(0, B) as b:
                for c in range(KC):
                    hold(added, 16 * (KC * b + c + 1))
                    sp.dma_start(basis[:, bass.ds(b, 1), c, :],
                                 basis1[bass.ds(b, 1), c * P:(c + 1) * P, :].rearrange("b p d -> p b d"))\
                      .then_inc(basis_in[1], 16)

            def load_c_table(i, s):
                load(C.x, C.x_in, acc1_nodes, D, i, s)

            def load_c_other(i, s):
                load(C.other, C.other_in, x_nodes, D, i, s)

            def load_c(i, s):
                load_c_table(i, s)
                load_c_other(i, s)

            sp.wait_ge(split_lo, 2 + KC)
            for s in range(XS):
                load_c_other(0, s)
            sp.wait_ge(added, 16 * ET)
            for s in range(XS):
                load_c_table(0, s)
            sp.wait_ge(cleared, 2)

            def done_c(q):
                hold(dis_put, q + 1)
                hold(evac_v, C.evac0 + GT * q + GT)

            def release_c(q):
                hold(turned, C.tile0 + GT * q + GT)
                hold(evac_v, C.evac0 + GT * q + GT)

            node_pass(C, load_c, release_c, lambda i, s: store(C, acc2_nodes, WIDE, i, s), done_c)

            def load_z_table(i, s):
                load(Z.x, Z.x_in, acc2_nodes, WIDE, i, s)

            def load_z_other(i, s):
                load(Z.other, Z.other_in, acc3_nodes, D, i, s)

            def load_z(i, s):
                load_z_table(i, s)
                load_z_other(i, s)

            sp.wait_ge(ring_cleared, 1 + U)
            sp.wait_ge(added, 16 * 2 * ET)
            for s in range(len(Z.x)):
                load_z_table(0, s)
            sp.wait_ge(added, 16 * 3 * ET)
            for s in range(len(Z.x)):
                load_z_other(0, s)

            def done_z(q):
                hold(finished, GT * q + GT)

            node_pass(Z, load_z, done_z, lambda i, s: store(Z, out_nodes, D, i, s), done_z)
            sp.wait_ge(tables_zeroed, 16 * (3 + 2 * NT // GT))
            for s in range(OS):
                sp.wait_ge(stored[s], 32 * (NT // GT // OS) * 2)
            for s in range(2 * OS):
                sp.wait_ge(z_stored[s], 32 * (NT // GT // OS // 2))

        @block.gpsimd
        def _(pool):
            pool.memset(zeros[:, :], 0.0).then_inc(cleared, 1)
            pool.memset(oring[:, :, :, D:WIDE], 0.0).then_inc(cleared, 1)
            pool.iota(iota_i[:, :], pattern=[[1, P]], base=0, channel_multiplier=0).then_inc(pool_const, 1)
            pool.iota(spare_i[:, :], pattern=[[1, 1]], base=N, channel_multiplier=1).then_inc(pool_const, 1)
            pool.memset(ones[:, :], 1.0).then_inc(pool_const, 1)
            pool.memset(ident[:, :], 0.0).then_inc(pool_const, 1)
            pool.wait_ge(pool_const, 4)
            pool.affine_select(out=ident[:, :], in_=ident[:, :], compare_op=ALU.not_equal, fill=1.0,
                               base=0, pattern=[[-1, P]], channel_multiplier=1).then_inc(pool_const, 1)
            pool.affine_select(out=before[:, :], in_=ones[:, :], compare_op=ALU.is_gt, fill=0.0,
                               base=0, pattern=[[1, P]], channel_multiplier=-1).then_inc(pool_const, 1)
            for n in range(ET // 4):
                pool.wait_ge(same_done, n + 1)
                wait(pool, counted, n - 1)
                pool.affine_select(out=low[n % 2], in_=same[:, 4 * n:4 * n + 4, :], compare_op=ALU.is_gt,
                                   fill=0.0, base=0, pattern=[[0, 4], [-1, P]], channel_multiplier=1)\
                    .then_inc(lower_done, 1)

            def hold(condition, value):
                pool.wait_ge(condition, value)
                if not isinstance(value, int):
                    pool.sem_inc(pool_turn, 1)

            def edge_pass(ep, table, width, sums, sum_width, ready):
                def step(i, k):
                    g = i * U + k + 5
                    if inside(g, ET):
                        s = (k + 5) % GS
                        pool.tensor_copy(index_now[:, (k + 5) % U, :], index[:, bass.ds(g, 1), :]
                                         .rearrange("p a b -> p (a b)")).then_inc(index_put, 1)
                        hold(index_put, ep.number * ET + g + 1)
                        if not isinstance(g, int) or g >= GS:
                            hold(normed, ep.norm0 + g - GS + 1)
                            hold(mixed, ep.number * ET + g - GS + 1)
                        pool.indirect_dma_start(
                            rows[:, s, 0:width], None, table,
                            bass.IndirectOffsetOnAxis(ap=index_now[:, (k + 5) % U, 0:1], axis=0))\
                            .then_inc(gathered[s], 16)
                    t = i * U + k
                    if inside(t, ET):
                        if ep is Fp:
                            hold(evac_v, ep.evac0 + t + 1)
                        else:
                            hold(evac_s, ep.evac0 + t + 1)
                        if isinstance(t, int) and t == 0:
                            ready()
                        else:
                            hold(added, 16 * (ep.number * ET + t))
                        pool.indirect_dma_start(
                            sums, bass.IndirectOffsetOnAxis(ap=index_now[:, k % U, 1:2], axis=0),
                            msgs[:, k % MS, 0:sum_width], None, compute_op=ALU.add).then_inc(added, 16)

                steps(pool, ET, U, 5, step)

            pool.sem_inc(rel_summed, 2)
            pool.sem_inc(rel_free, 2)

            def combine(layer, i, k):
                at = (i - 1) * (2 * KC * D)
                if k in sum_at[layer]:
                    kc = sum_at[layer][k]
                    n = BLOCKS * layer + (i - 1) * KC + kc
                    hold(bases_added, 2 * n + 2)
                    hold(rel_free, n + 1)
                    pool.tensor_tensor(combined[:, kc % 2, :], term[kc % 2][0], term[kc % 2][1], ALU.add)\
                        .then_inc(rel_summed, 1)
                if k in low_at[layer]:
                    kc = low_at[layer][k]
                    n = BLOCKS * layer + (i - 1) * KC + kc
                    hold(rel_high, n + 1)
                    pool.tensor_tensor(rel_w[:, bass.ds(at + (KC + kc) * D, D)], combined[:, kc % 2, :],
                                       rel_w[:, bass.ds(at + kc * D, D)], ALU.subtract).then_inc(rel_free, 1)

            with pool.Fori(1, R + 1) as i:
                for k in range(U):
                    combine(0, i, k)

            pool.wait_ge(graph_ready, 3)

            def ready_b():
                pool.wait_ge(tables_zeroed, 16 * (3 + 2 * NT // GT))
                for s in range(OS):
                    pool.wait_ge(stored[s], 32 * (NT // GT // OS))

            edge_pass(Bp, x, D, acc1, D, ready_b)

            def step_c(i, k):
                a = i * U + k + 2
                if k % GT == 0 and inside(a, NT):
                    q = (k + 2) % U // GT
                    hold(C.other_in[q], 32 * (i + (k + 2) // U + 1))
                    pool.tensor_tensor(gring[:, q, :, :], gring[:, q, :, :],
                                       bias[1][:, :].unsqueeze(1).to_broadcast([P, GT, D]), ALU.add)\
                        .then_inc(g_biased, 1)
                if not isinstance(i, int):
                    combine(1, i, k)
                if k % GT == 1 and k > 0:
                    q = k // GT
                    hold(stored[q % OS], 32 * (NT // GT // OS + i * (XS // OS) + q // OS))
                    pool.tensor_copy(oring[:, q % OS, :, D:D + 1],
                                     dis[:, bass.ds((i * XS + q) * GT, GT)].unsqueeze(2)).then_inc(dis_put, 1)

            steps(pool, NT, U, 2, step_c)

            def ready_d():
                pool.wait_ge(message_ends, 1)
                for s in range(OS):
                    pool.wait_ge(stored[s], 32 * 2 * (NT // GT // OS))

            pool.wait_ge(added, 16 * ET)
            edge_pass(Dp, acc1, D, acc2, WIDE, ready_d)

            pool.wait_ge(added, 16 * 2 * ET)
            edge_pass(Fp, acc2, WIDE, acc3, D, lambda: pool.wait_ge(tables_zeroed, 16 * (3 + 2 * NT // GT)))

            def step_z(i, k):
                t = i * Z.unroll + k
                if inside(t, NT):
                    q, j = k // GT, k % GT
                    if j == 0:
                        hold(Z.other_in[q], 32 * (i + 1))
                    hold(bias_scaled, t + 1)
                    pool.tensor_tensor(Z.other[q][:, j, :], Z.other[q][:, j, :], scaled_bias[:, k % 4, :], ALU.add)\
                        .then_inc(g_biased, 1)
                if inside(t - 2, NT):
                    q, j = (k - 2) % Z.unroll // GT, k % GT
                    hold(rectified, t - 1)
                    o = Z.results[q % len(Z.results)][:, j, 0:D]
                    pool.tensor_tensor(o, o, Z.x[q][:, j, 0:D], ALU.add).then_inc(finished, 1)

            steps(pool, NT, Z.unroll, 0, step_z, tail=2)

        @block.scalar
        def _(sc):
            sc.wait_ge(loops_in[0], 16)
            sc.activation(node_w[0][:, 0, :, :], raw[0], ACT.Copy, scale=SCALE).then_inc(split_hi, 1)
            sc.wait_ge(loops_in[1], 16)
            sc.activation(node_w[1][:, 0, :, :], raw[1], ACT.Copy, scale=SCALE).then_inc(split_hi, 1)
            sc.wait_ge(deg_std, 1)
            sc.activation(dis[:, :], dis[:, :], ACT.Sqrt).then_inc(deg_std, 1)

            def std_unit(pp, n, col, width):
                per = width
                sc.wait_ge(moment, pp.ln0 + per * n + per)
                sc.activation(std[:, col:col + width], moments[:, col:col + width, 1], ACT.Sqrt,
                              bias=eps[:, 0:1]).then_inc(deviation, 1)

            def split_high(pp, t, k):
                sc.wait_ge(turned, pp.tile0 + t + 1)
                wait(sc, product, pp.tile0 + t - 1)
                sc.activation(actT[:, k % 2, 0, :], psT[:, k % 2, :], ACT.Relu if pp is C else ACT.Copy)\
                  .then_inc(hi_done, 1)

            def hold(condition, value):
                sc.wait_ge(condition, value)
                sc.sem_inc(act_turn, 1)

            def scale_bases(layer, i, kc):
                n = BLOCKS * layer + (i - 1) * KC + kc
                if kc == 0:
                    sc.wait_ge(basis_in[layer], 16 * B * (KC if layer else 1))
                hold(rel_summed, n + 1)
                for h in range(2):
                    sc.activation(term[kc % 2][h], basis[:, 2 * h, kc, :], ACT.Copy,
                                  scale=comp[layer][:, bass.ds((i - 1) * B + 2 * h, 1)]).then_inc(bases_scaled, 1)

            def round_block(layer, i, kc):
                n = BLOCKS * layer + (i - 1) * KC + kc
                hold(rel_summed, n + 3)
                sc.activation(rel_w[:, bass.ds((i - 1) * (2 * KC * D) + kc * D, D)], combined[:, kc % 2, :], ACT.Copy)\
                  .then_inc(rel_high, 1)

            def node_step(pp, i, k):
                t = i * pp.unroll + k
                if inside(t + 1, NT):
                    split_high(pp, t + 1, k + 1)
                a = t + 2
                if pp.ln0 is not None and inside(a, NT):
                    c = (k + 2) % U
                    q, j = (k + 2) % pp.unroll // GT, k % GT
                    if j == 0:
                        sc.wait_ge(shift, pp.unit0 + i * (pp.unroll // GT) + (k + 2) // GT + 1)
                    wait(sc, turned, pp.tile0 + a - 1)
                    sc.activation(act[:, c % 2, :], pp.x[q][:, j, 0:D], ACT.Relu,
                                  scale=rstd[:, c:c + 1], bias=nmean[:, c:c + 1]).then_inc(normed, 1)
                    if pp is Z:
                        if not isinstance(a, int) or a >= 4:
                            sc.wait_ge(g_biased, NT // GT + a - 3)
                        sc.activation(scaled_bias[:, c % 4, :], bias[2][:, :], ACT.Copy,
                                      scale=pp.x[q][:, j, D:D + 1]).then_inc(bias_scaled, 1)
                if pp is Z and inside(t - 2, NT):
                    q, j = (k - 2) % pp.unroll // GT, k % GT
                    sc.wait_ge(evac_v, pp.evac0 + t - 1)
                    o = pp.results[q % len(pp.results)][:, j, 0:D]
                    sc.activation(o, o, ACT.Relu, scale=pp.x[q][:, j, D:D + 1]).then_inc(rectified, 1)
                e = k + pp.ahead - 1
                if pp.ln0 is not None and k % GT == 1 and inside(t + pp.ahead - 1, NT):
                    std_unit(pp, i * (pp.unroll // GT) + e // GT, e % U, GT)
                if pp is not Z and not isinstance(i, int):
                    layer = pp.number
                    if k in round_at[layer]:
                        round_block(layer, i, round_at[layer][k])
                    if k in scale_at[layer]:
                        scale_bases(layer, i, scale_at[layer][k])

            def edge_step(ep, i, k):
                h = i * U + k + 1
                if inside(h, ET):
                    split_high(ep, h, k + 1)
                b = i * U + k + 2
                if inside(b, ET):
                    c = (k + 2) % U
                    s = c % GS
                    wait(sc, turned, ep.tile0 + b - 1)
                    if ep.ln0 is not None:
                        sc.wait_ge(shift, ep.unit0 + b + 1)
                        sc.activation(act[:, c % 2, :], rows[:, s, 0:D], ACT.Relu,
                                      scale=rstd[:, c:c + 1], bias=nmean[:, c:c + 1]).then_inc(normed, 1)
                    else:
                        sc.wait_ge(gathered[s], 16 * (ep.number * ET // GS + i * (U // GS) + (k + 2) // GS + 1))
                        sc.activation(act[:, c % 2, :], rows[:, s, 0:D], ACT.Relu).then_inc(normed, 1)
                a = i * U + k + 3
                if ep.ln0 is not None and inside(a, ET):
                    std_unit(ep, a, (k + 3) % U, 1)
                if ep is Bp and isinstance(i, int) and i == 0 and 0 <= k < KC:
                    sc.wait_ge(loops_in[2], 16)
                    sc.wait_ge(product, A.tile0 + NT)
                    sc.activation(node_w[0][:, 0, k, :], raw[0][:, k, :], ACT.Copy, scale=SCALE)\
                      .then_inc(split_hi, 1)
                t = i * U + k - 1
                if ep is not Fp and inside(t, ET):
                    sc.wait_ge(product, ep.tile0 + t + 1)
                    wait(sc, added, 16 * (ep.number * ET + t - MS + 1))
                    sc.activation(msgs[:, (k - 1) % MS, 0:D], psZ[:, (k - 1) % ZS, :], ACT.Copy, scale=1.0 / SCALE)\
                      .then_inc(evac_s, 1)

            sc.wait_ge(comp_scaled, 2)
            steps(sc, NT, U, A.ahead, lambda i, k: node_step(A, i, k))
            steps(sc, ET, U, 3, lambda i, k: edge_step(Bp, i, k), tail=1)
            sc.wait_ge(added, 16 * ET)
            steps(sc, NT, U, 1, lambda i, k: node_step(C, i, k))
            steps(sc, ET, U, 3, lambda i, k: edge_step(Dp, i, k), tail=1)
            steps(sc, ET, U, 3, lambda i, k: edge_step(Fp, i, k))
            steps(sc, NT, Z.unroll, Z.ahead, lambda i, k: node_step(Z, i, k), tail=2)

        @block.vector
        def _(v):
            done = [0]

            def link(ins):
                done[0] += 1
                ins.then_inc(setup, 1)
                v.wait_ge(setup, done[0])

            v.memset(xring[96:P, :, :, :], 0.0).then_inc(ring_cleared, 1)
            link(v.memset(eps[:, :], EPS))
            v.wait_ge(pool_const, 6)
            v.tensor_copy(iota[:, :], iota_i[:, :]).then_inc(setup, 1)
            done[0] += 1
            link(v.tensor_copy(spare[:, :], spare_i[:, :]))
            link(v.tensor_scalar(iota_nt[:, :], iota[:, :], float(NT), None, ALU.mult))

            def split_low(n, slot, weights):
                v.wait_ge(split_hi, n + 1)
                v.scalar_tensor_tensor(out=weights[:, 1, :, :].rearrange("p c d -> p (c d)"),
                                       in0=raw[slot].rearrange("p c d -> p (c d)"), scalar=SCALE,
                                       in1=weights[:, 0, :, :].rearrange("p c d -> p (c d)"),
                                       op0=ALU.mult, op1=ALU.subtract).then_inc(split_lo, 1)

            split_low(0, 0, node_w[0])
            split_low(1, 1, node_w[1])

            v.wait_ge(edges_in, 64)
            link(v.tensor_copy(edge_f[0:EP, :, :], edge_i[0:EP, :, :]))
            link(v.tensor_tensor(mask3, edge_f[0:EP, 2, :].unsqueeze(1).to_broadcast([EP, R, EC]),
                                 iota[0:EP, 0:R].unsqueeze(2).to_broadcast([EP, R, EC]), ALU.is_equal))
            link(v.tensor_tensor_scan(run, ones[0:EP, 0:1].to_broadcast([EP, R * EC]), mask, 0.0,
                                      ALU.mult, ALU.add))
            link(v.tensor_copy(counts[0:EP, 0, :], run3[:, :, EC - 1]))
            link(v.tensor_tensor(run3[:, 1:R, :], run3[:, 1:R, :],
                                 counts[0:EP, 0, 0:R - 1].unsqueeze(2).to_broadcast([EP, R - 1, EC]), ALU.subtract))
            link(v.tensor_copy(counts[0:EP, 1, :], run3[:, :, EC - 1]))
            counted_here = done[0]
            v.wait_ge(setup_pe, 1)
            link(v.tensor_scalar(counts_i[:, :], psB[:, 1, 0:R], float(P - 1), None, ALU.add))
            link(v.tensor_scalar(counts_i[:, :], counts_i[:, :], 7, None, ALU.arith_shift_right))
            link(v.tensor_copy(counts[:, 2, :], counts_i[:, :]))
            link(v.tensor_tensor_scan(counts[:, 3, :], ones[:, 0:R], counts[:, 2, :], 0.0, ALU.mult, ALU.add))
            link(v.tensor_tensor(counts[:, 4, :], counts[:, 3, :], counts[:, 2, :], ALU.subtract))
            link(v.scalar_tensor_tensor(out=counts[:, 5, :], in0=counts[:, 4, :], scalar=float(P),
                                        in1=psB[:, 0, 0:R], op0=ALU.mult, op1=ALU.add))
            link(v.tensor_tensor(run3, run3, counts[0:EP, 5, :].unsqueeze(2).to_broadcast([EP, R, EC]), ALU.add))
            link(v.tensor_tensor(mask3, mask3, run3, ALU.mult))
            link(v.tensor_reduce(place[0:EP, 0, :], mask3.rearrange("p r c -> p c r"), AX_X, ALU.add))
            link(v.tensor_scalar(place_i[0:EP, 0, :], place[0:EP, 0, :], -1.0, None, ALU.add))
            link(v.tensor_scalar(place_i[0:EP, 1, :], place_i[0:EP, 0, :], 7, None, ALU.arith_shift_right))
            link(v.tensor_scalar(place_i[0:EP, 2, :], place_i[0:EP, 0, :], P - 1, None, ALU.bitwise_and))
            link(v.tensor_copy(place[0:EP, 1:3, :], place_i[0:EP, 1:3, :]))

            last_rel = act[:, 0, 0:ET * R].rearrange("p (t r) -> p t r", t=ET)
            link(v.tensor_tensor(last_rel, counts[:, 3, :].unsqueeze(1).to_broadcast([P, ET, R]),
                                 iota[:, 0:ET].unsqueeze(2).to_broadcast([P, ET, R]), ALU.is_le))
            link(v.tensor_reduce(flag[:, 0, :], last_rel, AX_X, ALU.add))
            v.tensor_scalar(tile_rel[:, :], flag[:, 0, :], float(R - 1), None, ALU.min).then_inc(graph_ready, 1)

            for n in range(CHUNKS):
                c0 = n * CH
                wait(v, picked_used, n - 1)
                v.tensor_tensor(hotJ[n % 2], iota[0:EP, :].unsqueeze(1).to_broadcast([EP, CH, P]),
                                place[0:EP, 2, c0:c0 + CH].unsqueeze(2).to_broadcast([EP, CH, P]),
                                ALU.is_equal).then_inc(picked, 1)
                v.tensor_tensor(hotR[n % 2][:, :, 3, :], iota[0:EP, 0:ET].unsqueeze(1).to_broadcast([EP, CH, ET]),
                                place[0:EP, 1, c0:c0 + CH].unsqueeze(2).to_broadcast([EP, CH, ET]),
                                ALU.is_equal).then_inc(picked, 1)
                v.wait_ge(picked, 5 * n + 2)
                for f, a in enumerate((edge_f[0:EP, 0, :], edge_f[0:EP, 1, :], edge_w[0:EP, :])):
                    v.tensor_tensor(hotR[n % 2][:, :, f, :], hotR[n % 2][:, :, 3, :],
                                    a[:, c0:c0 + CH].unsqueeze(2).to_broadcast([EP, CH, ET]), ALU.mult)\
                     .then_inc(picked, 1)
            v.wait_ge(picked_used, CHUNKS)
            link(v.tensor_copy(rec[:, :, :].rearrange("p f t -> p (f t)"), psB[:, 2, 0:4 * ET]))
            link(v.tensor_scalar(flag[:, 0, :], rec[:, 3, :], -1.0, 1.0, ALU.mult, ALU.add))
            link(v.scalar_tensor_tensor(out=rec[:, 1, :], in0=flag[:, 0, :], scalar=spare[:, 0:1],
                                        in1=rec[:, 1, :], op0=ALU.mult, op1=ALU.add))
            def compare(n):
                v.wait_ge(spread_pe, n + 1)
                v.tensor_tensor(same[:, 4 * n:4 * n + 4, :],
                                psB[:, n % 2, :].rearrange("p (t j) -> p t j", t=4),
                                rec[:, 1, 4 * n:4 * n + 4].unsqueeze(2).to_broadcast([P, 4, P]),
                                ALU.is_equal).then_inc(same_done, 1)

            def count(n):
                v.wait_ge(lower_done, n + 1)
                v.tensor_reduce(flag[:, 1, 4 * n:4 * n + 4], low[n % 2], AX_X, ALU.add).then_inc(counted, 1)

            for n in range(ET // 4 + 2):
                if n < ET // 4:
                    wait(v, spread_pe, n - 1)
                    v.tensor_tensor(diag[n % 2], ident[:, :].unsqueeze(1).to_broadcast([P, 4, P]),
                                    rec[:, 1, 4 * n:4 * n + 4].unsqueeze(2).to_broadcast([P, 4, P]),
                                    ALU.mult).then_inc(spread, 1)
                if 1 <= n <= ET // 4:
                    compare(n - 1)
                if n >= 2:
                    count(n - 2)
            v.wait_ge(counted, ET // 4)
            link(v.tensor_scalar(flag[:, 1, :], flag[:, 1, :], 0.5, None, ALU.is_gt))
            link(v.tensor_scalar(flag[:, 2, :], rec[:, 1, :], spare[:, 0:1], None, ALU.subtract))
            link(v.tensor_tensor(flag[:, 2, :], flag[:, 2, :], flag[:, 1, :], ALU.mult))
            link(v.tensor_tensor(flag[:, 2, :], rec[:, 1, :], flag[:, 2, :], ALU.subtract))
            v.tensor_copy(index[:, :, 1], flag[:, 2, :]).then_inc(setup, 1)
            done[0] += 1
            v.tensor_copy(index[:, :, 0], rec[:, 0, :]).then_inc(graph_ready, 1)

            for n in range(CHUNKS):
                c0 = n * CH
                b = n % 2
                wait(v, deg_used, n - 1)
                v.tensor_tensor(reach[b], iota_nt[0:EP, :].unsqueeze(1).to_broadcast([EP, CH, P]),
                                edge_f[0:EP, 0, c0:c0 + CH].unsqueeze(2).to_broadcast([EP, CH, P]),
                                ALU.is_le).then_inc(deg_hot, 1)
                v.wait_ge(deg_hot, 7 * n + 1)
                v.tensor_reduce(place[0:EP, 3, c0:c0 + CH], reach[b], AX_X, ALU.add).then_inc(deg_hot, 1)
                v.wait_ge(deg_hot, 7 * n + 2)
                v.tensor_scalar(place[0:EP, 4, c0:c0 + CH], place[0:EP, 3, c0:c0 + CH], -float(NT), float(NT),
                                ALU.mult, ALU.add).then_inc(deg_hot, 1)
                v.wait_ge(deg_hot, 7 * n + 3)
                v.tensor_tensor(place[0:EP, 4, c0:c0 + CH], place[0:EP, 4, c0:c0 + CH],
                                edge_f[0:EP, 0, c0:c0 + CH], ALU.add).then_inc(deg_hot, 1)
                v.tensor_scalar(place[0:EP, 3, c0:c0 + CH], place[0:EP, 3, c0:c0 + CH], -1.0, None, ALU.add)\
                 .then_inc(deg_hot, 1)
                v.wait_ge(deg_hot, 7 * n + 5)
                v.tensor_tensor(hotT[b], iota[0:EP, 0:NT].unsqueeze(1).to_broadcast([EP, CH, NT]),
                                place[0:EP, 4, c0:c0 + CH].unsqueeze(2).to_broadcast([EP, CH, NT]),
                                ALU.is_equal).then_inc(deg_hot, 1)
                v.tensor_tensor(hotQ[b], iota[0:EP, :].unsqueeze(1).to_broadcast([EP, CH, P]),
                                place[0:EP, 3, c0:c0 + CH].unsqueeze(2).to_broadcast([EP, CH, P]),
                                ALU.is_equal).then_inc(deg_hot, 1)
            v.wait_ge(deg_used, CHUNKS)
            v.tensor_scalar(dis[:, :], psB[:, 1, 0:NT], 1.0, None, ALU.add).then_inc(deg_std, 1)
            v.wait_ge(deg_std, 2)
            v.reciprocal(dis[:, :], dis[:, :]).then_inc(graph_ready, 1)
            v.wait_ge(consts_in, 80)
            for n in range(2):
                v.tensor_scalar(comp[n][:, :], comp[n][:, :], SCALE, None, ALU.mult).then_inc(comp_scaled, 1)
            v.wait_ge(comp_scaled, 2)

            def add_bases(layer, i, kc):
                n = BLOCKS * layer + (i - 1) * KC + kc
                for h in range(2):
                    v.wait_ge(bases_scaled, 2 * n + h + 1)
                    v.scalar_tensor_tensor(out=term[kc % 2][h], in0=basis[:, 2 * h + 1, kc, :],
                                           scalar=comp[layer][:, bass.ds((i - 1) * B + 2 * h + 1, 1)],
                                           in1=term[kc % 2][h], op0=ALU.mult, op1=ALU.add).then_inc(bases_added, 1)

            def tile_moments(pp, t, c):
                v.wait_ge(stat, pp.ln0 + t + 1)
                if not isinstance(t, int):
                    v.sem_inc(dve_turn, 1)
                v.bn_aggr(moments[:, c, :], stats[:, c, :]).then_inc(moment, 1)

            def scale_of(pp, unit, c, w):
                v.wait_ge(deviation, pp.unit0 + unit + 1)
                v.reciprocal(rstd[:, c:c + w], std[:, c:c + w]).then_inc(inverse, 1)

            def shift_of(pp, unit, c, w, degrees=None):
                v.wait_ge(inverse, pp.unit0 + unit + 1)
                if degrees is not None:
                    v.tensor_tensor(rstd[:, c:c + w], rstd[:, c:c + w], degrees, ALU.mult).then_inc(inverse_d, 1)
                    v.wait_ge(inverse_d, unit + 1)
                v.scalar_tensor_tensor(out=nmean[:, c:c + w], in0=moments[:, c:c + w, 0], scalar=-1.0,
                                       in1=rstd[:, c:c + w], op0=ALU.mult, op1=ALU.mult).then_inc(shift, 1)

            def split_lower(pp, t, k):
                v.wait_ge(hi_done, pp.tile0 + t + 1)
                s = k % 2
                if pp is C:
                    ins = v.scalar_tensor_tensor(out=actT[:, s, 1, :], in0=psT[:, s, :], scalar=0.0,
                                                 in1=actT[:, s, 0, :], op0=ALU.max, op1=ALU.subtract)
                else:
                    ins = v.tensor_tensor(actT[:, s, 1, :], psT[:, s, :], actT[:, s, 0, :], ALU.subtract)
                ins.then_inc(lo_done, 1)

            def node_step(pp, i, k):
                layernorm = pp.ln0 is not None
                t = i * pp.unroll + k
                e = k + pp.ahead - 2
                new_unit = layernorm and k % GT == 0 and inside(t + pp.ahead - 2, NT)
                unit = i * (pp.unroll // GT) + e // GT
                if new_unit:
                    scale_of(pp, unit, e % U, GT)
                if layernorm and inside(t + pp.ahead, NT):
                    q, j = (k + pp.ahead) % pp.unroll // GT, k % GT
                    if j == 0:
                        v.wait_ge(pp.x_in[q], 32 * (pp.x_before + i + (k + pp.ahead) // pp.unroll + 1))
                    v.bn_stats(stats[:, (k + pp.ahead) % U, :], pp.x[q][:, j, 0:D]).then_inc(stat, 1)
                if new_unit:
                    shift_of(pp, unit, e % U, GT,
                             pp.x[e % pp.unroll // GT][:, :, D:D + 1].rearrange("p g o -> p (g o)")
                             if pp is Z else None)
                if inside(t + 1, NT):
                    split_lower(pp, t + 1, k + 1)
                if layernorm and inside(t + pp.ahead, NT):
                    tile_moments(pp, t + pp.ahead, (k + pp.ahead) % U)
                if inside(t - 1, NT):
                    q, j = (k - 1) % pp.unroll // GT, (k - 1) % GT
                    slots = len(pp.results)
                    if j == 0:
                        wait(v, pp.stored[q % slots], 32 * (pp.stores_before + i * (len(pp.x) // slots)
                                                            + (k - 1) // GT // slots))
                    v.wait_ge(product, pp.tile0 + t)
                    if pp is A:
                        addend = bias[0][:, :]
                    else:
                        addend = pp.other[q][:, j, :]
                        v.wait_ge(g_biased, i * (U // GT) + (k - 1) // GT + 1 if pp is C else NT // GT + t)
                    v.scalar_tensor_tensor(out=pp.results[q % slots][:, j, 0:D], in0=psZ[:, (k - 1) % ZS, :],
                                           scalar=1.0 / SCALE, in1=addend,
                                           op0=ALU.mult, op1=ALU.add).then_inc(evac_v, 1)
                if pp is not Z and not isinstance(i, int) and k in scale_at[pp.number]:
                    add_bases(pp.number, i, scale_at[pp.number][k])

            def edge_step(ep, i, k):
                layernorm = ep.ln0 is not None
                a = i * U + k + 3
                b = i * U + k + 2
                c = (k + 2) % U
                s = c % GS
                if layernorm and inside(b, ET):
                    scale_of(ep, b, c, 1)
                if layernorm and inside(a, ET):
                    v.wait_ge(gathered[(k + 3) % GS],
                              16 * (ep.number * ET // GS + i * (U // GS) + (k + 3) // GS + 1))
                    v.bn_stats(stats[:, (k + 3) % U, :], rows[:, (k + 3) % GS, 0:D]).then_inc(stat, 1)
                if layernorm and inside(b, ET):
                    shift_of(ep, b, c, 1)
                h = i * U + k + 1
                if inside(h, ET):
                    split_lower(ep, h, k + 1)
                if layernorm and inside(a, ET):
                    tile_moments(ep, a, (k + 3) % U)
                if inside(b, ET):
                    wait(v, turned, ep.tile0 + b - 1)
                    if ep is Fp:
                        v.tensor_scalar(mix[:, c % 2, :], same[:, bass.ds(b, 1), :].rearrange("p a j -> p (a j)"),
                                        rows[:, s, D:D + 1], rec[:, 3, bass.ds(b, 1)], ALU.mult, ALU.mult)\
                         .then_inc(mixed, 1)
                    else:
                        v.tensor_scalar(mix[:, c % 2, :], same[:, bass.ds(b, 1), :].rearrange("p a j -> p (a j)"),
                                        rec[:, 2, bass.ds(b, 1)], None, ALU.mult).then_inc(mixed, 1)
                if ep is Bp and isinstance(i, int) and i == 0 and 0 <= k < KC:
                    v.wait_ge(split_hi, 2 + k + 1)
                    v.scalar_tensor_tensor(out=node_w[0][:, 1, k, :], in0=raw[0][:, k, :], scalar=SCALE,
                                           in1=node_w[0][:, 0, k, :], op0=ALU.mult, op1=ALU.subtract)\
                     .then_inc(split_lo, 1)
                if ep is Fp and isinstance(i, int) and i == ET // U - 1 and k < U:
                    v.memset(over_w[k], 0.0).then_inc(ring_cleared, 1)
                if ep is Fp:
                    t = i * U + k - 1
                    if inside(t, ET):
                        v.wait_ge(product, ep.tile0 + t + 1)
                        wait(v, added, 16 * (ep.number * ET + t - MS + 1))
                        v.wait_ge(bias_row, t + 1)
                        v.scalar_tensor_tensor(out=msgs[:, (k - 1) % MS, 0:D], in0=psZ[:, (k - 1) % ZS, :],
                                               scalar=1.0 / SCALE, in1=bias_rows[:, (k - 1) % 2, :],
                                               op0=ALU.mult, op1=ALU.add).then_inc(evac_v, 1)
                    if inside(h, ET):
                        v.wait_ge(turned, ep.tile0 + h + 1)
                        wait(v, evac_v, ep.evac0 + h - 1 if not isinstance(h, int) or h >= 2 else 0)
                        v.tensor_scalar(bias_rows[:, (k + 1) % 2, :], bias[2][:, :], psS[:, (k + 1) % 2, 0:1], None,
                                        ALU.mult).then_inc(bias_row, 1)

            steps(v, NT, U, A.ahead, lambda i, k: node_step(A, i, k), tail=1)
            v.memset(msgs[:, :, D:WIDE], 0.0).then_inc(message_ends, 1)
            steps(v, ET, U, 3, lambda i, k: edge_step(Bp, i, k))
            steps(v, NT, U, 1, lambda i, k: node_step(C, i, k), tail=1)
            steps(v, ET, U, 3, lambda i, k: edge_step(Dp, i, k))
            steps(v, ET, U, 3, lambda i, k: edge_step(Fp, i, k), tail=1)
            steps(v, NT, Z.unroll, Z.ahead, lambda i, k: node_step(Z, i, k), tail=1)

        @block.tensor
        def _(pe):
            pe.wait_ge(setup, 10)
            pe.wait_ge(pool_const, 6)
            pe.matmul(psB[:, 0, 0:R], before[0:EP, :], counts[0:EP, 1, :], start=True, stop=True)
            pe.matmul(psB[:, 1, 0:R], ones[0:EP, :], counts[0:EP, 1, :], start=True, stop=True)\
              .then_inc(setup_pe, 1)
            for n in range(CHUNKS):
                pe.wait_ge(picked, 5 * n + 5)
                for c in range(CH):
                    last = pe.matmul(psB[:, 2, 0:4 * ET], hotJ[n % 2][:, c, :],
                                     hotR[n % 2][:, c, :, :].rearrange("p f t -> p (f t)"),
                                     start=(n == 0 and c == 0), stop=(n == CHUNKS - 1 and c == CH - 1))
                last.then_inc(picked_used, 1)
            for n in range(ET // 4):
                pe.wait_ge(spread, n + 1)
                wait(pe, same_done, n - 1)
                pe.matmul(psB[:, n % 2, :], ones[:, :], diag[n % 2].rearrange("p t j -> p (t j)"),
                          start=True, stop=True).then_inc(spread_pe, 1)
            pe.wait_ge(same_done, ET // 4)
            for n in range(CHUNKS):
                pe.wait_ge(deg_hot, 7 * n + 7)
                for c in range(CH):
                    last = pe.matmul(psB[:, 1, 0:NT], hotQ[n % 2][:, c, :], hotT[n % 2][:, c, :],
                                     start=(n == 0 and c == 0), stop=(n == CHUNKS - 1 and c == CH - 1))
                last.then_inc(deg_used, 1)

            def multiply(pp, t, k, weights):
                pe.wait_ge(lo_done, pp.tile0 + t + 1)
                s = k % 2
                for c in range(KC):
                    for part, half in ((0, 0), (0, 1), (1, 0)):
                        last = pe.matmul(psZ[:, k % ZS, :], actT[:, s, part, c * P:(c + 1) * P], weights(half, c),
                                         start=(c == 0 and part == 0 and half == 0), stop=(c == KC - 1 and part == 1))
                last.then_inc(product, 1)

            def slot_free(pp, t, evacuated):
                if not isinstance(t, int) or t >= ZS:
                    pe.wait_ge(evacuated, pp.evac0 + t - ZS + 1)
                elif pp in last_evacuation:
                    before, count = last_evacuation[pp]
                    pe.wait_ge(before, count - ZS + 1 + t)

            last_evacuation = {Bp: (evac_v, A.evac0 + NT), C: (evac_s, Bp.evac0 + ET), Dp: (evac_v, C.evac0 + NT),
                               Fp: (evac_s, Dp.evac0 + ET), Z: (evac_v, Fp.evac0 + ET)}

            def turn_slot_free(pp, t):
                wait(pe, lo_done, pp.tile0 + t - 1)

            def node_step(pp, i, k, w):
                a = i * pp.unroll + k + 1
                if inside(a, NT):
                    c = k + 1
                    q, j = (k + 1) % pp.unroll // GT, (k + 1) % GT
                    if pp is C:
                        if j == 0:
                            pe.wait_ge(pp.x_in[q], 32 * (pp.x_before + i + (k + 1) // pp.unroll + 1))
                        source = pp.x[q][:, j, 0:D]
                    else:
                        pe.wait_ge(normed, pp.norm0 + a + 1)
                        source = act[:, c % 2, :]
                    turn_slot_free(pp, a)
                    for n in range(KC):
                        last = pe.transpose(psT[:, c % 2, n * P:(n + 1) * P], source[:, n * P:(n + 1) * P], ident[:, :])
                    last.then_inc(turned, 1)
                t = i * pp.unroll + k
                if inside(t, NT):
                    slot_free(pp, t, evac_v)
                    multiply(pp, t, k, lambda half, c: w[:, half, c, :])

            def edge_step(ep, i, k):
                a = i * U + k + 1
                if inside(a, ET):
                    c = (k + 1) % U
                    pe.wait_ge(normed, ep.norm0 + a + 1)
                    pe.wait_ge(mixed, ep.number * ET + a + 1)
                    turn_slot_free(ep, a)
                    for n in range(KC):
                        last = pe.matmul(psT[:, c % 2, n * P:(n + 1) * P], act[:, c % 2, n * P:(n + 1) * P],
                                         mix[:, c % 2, :], start=True, stop=True)
                    if ep is Fp:
                        wait(pe, bias_row, a - 1)
                        last = pe.matmul(psS[:, c % 2, 0:1], mix[:, c % 2, :], ones[:, 0:1],
                                         start=True, stop=True)
                    last.then_inc(turned, 1)
                t = i * U + k
                if inside(t, ET):
                    if ep is Fp:
                        weights = lambda half, c: node_w[0][:, half, c, :]
                    else:
                        r = pe.value_load(tile_rel[0:1, bass.ds(t, 1)], min_val=0, max_val=R - 1)
                        weights = lambda half, c: rel_w[:, bass.ds(r * (2 * KC * D) + (half * KC + c) * D, D)]
                    slot_free(ep, t, evac_v if ep is Fp else evac_s)
                    multiply(ep, t, k, weights)

            pe.wait_ge(split_lo, 1)
            pe.wait_ge(deg_std, 1)
            steps(pe, NT, U, 1, lambda i, k: node_step(A, i, k, node_w[0]))
            pe.wait_ge(rel_free, BLOCKS + 2)
            pe.wait_ge(graph_ready, 1)
            steps(pe, ET, U, 1, lambda i, k: edge_step(Bp, i, k))
            pe.wait_ge(split_lo, 2)
            steps(pe, NT, U, 1, lambda i, k: node_step(C, i, k, node_w[1]))
            pe.wait_ge(rel_free, 2 * BLOCKS + 2)
            steps(pe, ET, U, 1, lambda i, k: edge_step(Dp, i, k))
            pe.wait_ge(split_lo, 2 + KC)
            steps(pe, ET, U, 1, lambda i, k: edge_step(Fp, i, k))
            steps(pe, NT, Z.unroll, 1, lambda i, k: node_step(Z, i, k, node_w[0]))


def kernel(x, src, dst, edge_type_8, edge_weight, L0_gnn_basis0, L0_gnn_comp0, L0_gnn_bias0, L0_gnn_loop0,
           L0_gnn_basis1, L0_gnn_comp1, L0_gnn_bias1, L0_gnn_loop1, L1_gnn_W, L1_gnn_b):
    import numpy as np
    import concourse.bacc as bacc
    from concourse.bass_utils import run_bass_kernel_spmd

    nc = bacc.Bacc("TRN2", target_bir_lowering=False, num_devices=1)
    inputs = [("x", x), ("src", src), ("dst", dst), ("etype", edge_type_8), ("weight", edge_weight),
              ("basis0", L0_gnn_basis0), ("comp0", L0_gnn_comp0), ("bias0", L0_gnn_bias0), ("loop0", L0_gnn_loop0),
              ("basis1", L0_gnn_basis1), ("comp1", L0_gnn_comp1), ("bias1", L0_gnn_bias1), ("loop1", L0_gnn_loop1),
              ("w2t", np.asarray(L1_gnn_W).T), ("bias2", L1_gnn_b)]
    arrays, args = {}, []
    for name, a in inputs:
        a = np.ascontiguousarray(a)
        arrays[f"in_{name}"] = a
        args.append(nc.dram_tensor(f"in_{name}", a.shape, mybir.dt.from_np(a.dtype), kind="ExternalInput").ap())
    out = nc.dram_tensor("out_x", tuple(x.shape), F32, kind="ExternalOutput").ap()
    gnn_kernel(nc, *args, out)
    r = run_bass_kernel_spmd(nc, [arrays], core_ids=[0])
    return r.results[0]["out_x"]
```

```python
from contextlib import ExitStack

import concourse.bass as bass
from concourse import mybir

P = 128
ALU = mybir.AluOpType
ACT = mybir.ActivationFunctionType
F32 = mybir.dt.float32
F16 = mybir.dt.float16
I32 = mybir.dt.int32
AX_X = mybir.AxisListType.X
EPS = 1e-5
SCALE = 64.0


def wait(eng, sem, value):
    if not isinstance(value, int) or value > 0:
        eng.wait_ge(sem, value)


def inside(t, count):
    return not isinstance(t, int) or 0 <= t < count


def steps(eng, tiles, unroll, lead, step, tail=0, before_last=None, after_last=None):
    for k in range(-lead, unroll):
        step(0, k)
    with eng.Fori(1, tiles // unroll - 1) as i:
        for k in range(unroll):
            step(i, k)
    last = tiles // unroll - 1
    for k in range(unroll):
        if before_last is not None:
            before_last(k - unroll)
        step(last, k)
        if k == unroll - 1:
            for drain in range(tail):
                step(last, unroll + drain)
        if after_last is not None:
            after_last(k - unroll)


def ahead_of(step, lead, at_once=0):
    def run(k):
        if k == at_once - lead:
            for j in range(-lead, k):
                step(0, j)
        if k >= at_once - lead:
            step(0, k)
    return run


def lags(i, k, lag, least):
    if not isinstance(i, int) or i == 0 or k < 0:
        return [lag]
    now = max(least, lag - k // 2)
    before = max(least, lag - (k - 1) // 2) if k > 0 else lag
    return list(range(before, now - 1, -1))


class NodePass:

    def __init__(self, number, tile0, evac0, norm0=None, ln0=None, unit0=None, unroll=8, ahead=4):
        self.number, self.tile0, self.evac0 = number, tile0, evac0
        self.norm0, self.ln0, self.unit0, self.unroll = norm0, ln0, unit0, unroll
        self.ahead = ahead

    def set_rings(self, x, x_in, x_base, x_unit, other, other_in, results, stored, stored_base, stored_unit):
        self.x, self.x_in, self.x_base, self.x_unit = x, x_in, x_base, x_unit
        self.other, self.other_in = other, other_in
        self.results, self.stored, self.stored_base, self.stored_unit = results, stored, stored_base, stored_unit


class EdgePass:

    def __init__(self, number, tile0, evac0, norm0, tiles, ln0=None, unit0=None):
        self.number, self.tile0, self.evac0, self.tiles = number, tile0, evac0, tiles
        self.norm0, self.ln0, self.unit0 = norm0, ln0, unit0

    def set_graph(self, same, index):
        self.same, self.index = same, index


def gnn_kernel(nc, x, src, dst, etype, weight, basis0, comp0, bias0, loop0,
               basis1, comp1, bias1, loop1, w2t, bias2, out):
    N, D = x.shape
    E = src.shape[0]
    R, B = comp0.shape
    KC = D // P
    NT = 80
    NP = N // NT
    GT = 2
    U = 8
    XS, OS = 4, 2
    EC = 40
    EP = E // EC
    ET = -(-((E + R * (P - 1)) // P) // U) * U
    GS, MS = XS * GT, 4
    FINISH = 7
    LEAD = 8
    WIDE = D + 4
    ROWS = P * NT
    FULL = NP // 16 * 16
    BLOCKS = R * KC
    ZS = 4
    assert NP * NT == N and EP * EC == E and NP <= P and EP <= P and N + P <= ROWS
    assert ET == 48 and EC % U == 0 and R == NT // U - 2 and B == 4

    acc1 = nc.dram_tensor("acc1", (ROWS, D), F32, kind="Internal").ap()
    acc2 = nc.dram_tensor("acc2", (ROWS, WIDE), F32, kind="Internal").ap()
    acc3 = nc.dram_tensor("acc3", (ROWS, D), F32, kind="Internal").ap()

    A = NodePass(0, 0, 0, norm0=0, ln0=0, unit0=0)
    Bp = EdgePass(0, NT, 0, NT, ET, ln0=NT, unit0=NT // GT)
    C = NodePass(1, NT + ET, NT)
    Dp = EdgePass(1, 2 * NT + ET, ET, NT + ET, ET)
    Fp = EdgePass(2, 2 * NT + 2 * ET, 2 * NT, NT + 2 * ET, EC, ln0=NT + ET, unit0=NT // GT + ET)
    Z = NodePass(2, Fp.tile0 + EC, 2 * NT + EC, norm0=Fp.norm0 + EC, ln0=Fp.ln0 + EC, unit0=Fp.unit0 + EC,
                 unroll=2 * U, ahead=6)

    with ExitStack() as ctx:
        def sb(name, shape, dt):
            return ctx.enter_context(nc.sbuf_tensor(name, shape, dt))

        def psum(name, shape):
            return ctx.enter_context(nc.psum_tensor(name, shape, F32))

        def sem(name):
            return ctx.enter_context(nc.semaphore(name))

        rel_w = sb("rel_w", [P, R * 2 * KC * D], F16)
        node_w = [sb(f"node_w{n}", [P, 2, KC, D], F16) for n in range(2)]
        basis = sb("basis", [P, B, KC, D], F32)
        combined = sb("combined", [P, 2, D], F32)
        comp = [sb(f"comp{n}", [P, R * B], F32) for n in range(2)]
        bias = [sb(f"bias{n}", [P, D], F32) for n in range(3)]
        bias_rows = basis[:, 1, :, :]
        xring = sb("xring", [P, XS, GT, WIDE], F32)
        gring = sb("gring", [P, XS, GT, D], F32)
        oring = sb("oring", [P, OS, GT, WIDE], F32)
        scaled_bias = basis[:, 0, :, :]
        rows = xring[:, :, :, :].rearrange("p s g d -> p (s g) d")
        edge_ring = sb("edge_ring", [P, 2 * MS * WIDE], F32)
        msgs = edge_ring[:, MS * WIDE:2 * MS * WIDE].rearrange("p (s d) -> p s d", s=MS)
        mix = sb("mix", [P, 2, P], F32)
        index_now = sb("index_now", [P, U, 2], I32)
        act = sb("act", [P, 2, D], F32)
        actT = sb("actT", [P, 2, 2, D], F16)
        parted = combined[:, :, :].bitcast(F16).rearrange("p s (h d) -> p s h d", h=2)
        stats = sb("stats", [P, U, 6], F32)
        moments = sb("moments", [P, U, 2], F32)
        std = sb("std", [P, U], F32)
        rstd = sb("rstd", [P, U], F32)
        nmean = sb("nmean", [P, U], F32)
        eps = sb("eps", [P, 1], F32)
        weight_sum = sb("weight_sum", [P, 2], F32)
        same = sb("same", [P, ET, P], F16)
        rec = sb("rec", [P, 4, ET], F32)
        index = sb("index", [P, ET, 2], I32)
        tile_rel = sb("tile_rel", [P, ET], I32)
        dis = sb("dis", [P, NT], F32)
        ident = sb("ident", [P, P], F32)
        ones = sb("ones", [P, P], F32)
        before = oring[:, 1, 1, 0:P]
        iota_i = oring[:, 1, 1, P:2 * P].bitcast(I32)
        iota = sb("iota", [P, P], F32)
        iota_nt = sb("iota_nt", [P, P], F32)
        iota1 = sb("iota1", [P, P], F32)
        spare_i = sb("spare_i", [P, 1], I32)
        spare = sb("spare", [P, 1], F32)
        zeros = sb("zeros", [P, WIDE], F32)
        edge_i = oring[:, 0, 0, 0:3 * EC].bitcast(I32).rearrange("p (n c) -> p n c", n=3)
        edge_w = sb("edge_w", [P, EC], F32)
        edge_f = sb("edge_f", [P, 3, EC], F32)
        counts = sb("counts", [P, 6, R], F32)
        counts_i = sb("counts_i", [P, R], I32)
        place = mix[:, 0, 0:3 * EC].rearrange("p (n c) -> p n c", n=3)
        place_i = oring[:, 0, 1, 0:3 * EC].bitcast(I32).rearrange("p (n c) -> p n c", n=3)
        flag = sb("flag", [P, 3, ET], F32)

        xs = [xring[:, s, :, :] for s in range(XS)]
        gs = [gring[:, s, :, :] for s in range(XS)]
        outs = [oring[:, s, :, :] for s in range(OS)]
        taken = [0]

        def over_rel_w(slots, width):
            found = []
            for _ in range(slots):
                a = taken[0]
                taken[0] = a + 2 * GT * width
                found.append(rel_w[:, a:a + 2 * GT * width].bitcast(F32).rearrange("p (g d) -> p g d", g=GT))
            return found

        z_xs = over_rel_w(2 * XS, WIDE)
        z_gs = gs + over_rel_w(XS, D)
        z_outs = outs + over_rel_w(OS, D) + xs
        assert taken[0] <= R * 2 * KC * D

        psT = psum("psT", [P, 2, D])
        psZ = psum("psZ", [P, ZS, D])
        psS = psum("psS", [P, 2, D])

        edges_in = sem("edges_in")
        consts_in = sem("consts_in")
        loops_in = [sem(f"loop_in{n}") for n in range(3)]
        basis_in = [sem(f"basis_in{n}") for n in range(2)]
        cleared = sem("cleared")
        pool_const = sem("pool_const")
        tables_zeroed = sem("tables_zeroed")
        graph_ready = sem("graph_ready")
        message_ends = sem("message_ends")
        ring_cleared = sem("ring_cleared")
        comp_scaled = sem("comp_scaled")
        act_turn = sem("act_turn")
        dve_turn = sem("dve_turn")
        sp_turn = sem("sp_turn")
        setup = sem("setup")
        setup_pe = sem("setup_pe")
        placed = sem("placed")
        picked = sem("picked")
        picked_used = sem("picked_used")
        recorded = sem("recorded")
        spread = sem("spread")
        spread_pe = sem("spread_pe")
        same_done = sem("same_done")
        lower_done = sem("lower_done")
        counted = sem("counted")
        dense_diag = sem("dense_diag")
        dense_pe = sem("dense_pe")
        dense_same = sem("dense_same")
        dense_low = sem("dense_low")
        dense_counted = sem("dense_counted")
        deg_added = sem("deg_added")
        deg_hot = sem("deg_hot")
        deg_used = sem("deg_used")
        deg_std = sem("deg_std")
        split_hi = sem("split_hi")
        split_lo = sem("split_lo")
        bases_scaled = sem("bases_scaled")
        bases_added = sem("bases_added")
        rel_summed = sem("rel_summed")
        rel_high = sem("rel_high")
        rel_free = sem("rel_free")
        x_in = [sem(f"x_in{s}") for s in range(XS)]
        g_in = [sem(f"g_in{s}") for s in range(XS)]
        stored = [sem(f"stored{s}") for s in range(OS)]
        z_in = [sem(f"z_in{s}") for s in range(2 * XS)]
        z_other_in = [sem(f"z_other_in{s}") for s in range(2 * XS)]
        z_stored = [sem(f"z_stored{s}") for s in range(2 * XS)]
        g_biased = sem("g_biased")
        bias_scaled = sem("bias_scaled")
        dis_put = sem("dis_put")
        gathered = [sem(f"gathered{s}") for s in range(GS)]
        index_put = sem("index_put")
        target_put = sem("target_put")
        pool_turn = sem("pool_turn")
        added = sem("added")
        stat = sem("stat")
        moment = sem("moment")
        deviation = sem("deviation")
        inverse = sem("inverse")
        inverse_d = sem("inverse_d")
        shift = sem("shift")
        normed = sem("normed")
        summed = sem("summed")
        rows_hi = sem("rows_hi")
        rows_lo = sem("rows_lo")
        mixed = sem("mixed")
        turned = sem("turned")
        hi_done = sem("hi_done")
        lo_done = sem("lo_done")
        product = sem("product")
        evac_v = sem("evac_v")
        evac_s = sem("evac_s")
        bias_row = sem("bias_row")
        third_added = sem("third_added")
        rectified = sem("rectified")
        finished = sem("finished")

        A.set_rings(xs, x_in, 0, 32, None, None, outs, stored, 0, 16)
        C.set_rings(xs, x_in, 32 * (NT // GT // XS), 16, gs, g_in, outs, stored, 16 * (NT // GT // OS), 16)
        Z.set_rings(z_xs, z_in, 0, 16, z_gs, z_other_in, z_outs, z_stored, 0, 32)

        by_node = "(p t) d -> p (t d)"
        x_nodes = x.rearrange(by_node, t=NT)
        out_nodes = out.rearrange(by_node, t=NT)
        acc1_nodes = acc1.rearrange(by_node, t=NT)
        acc2_nodes = acc2.rearrange(by_node, t=NT)
        acc3_nodes = acc3.rearrange(by_node, t=NT)
        PARTS = ((0, FULL), (FULL, NP))
        WHOLE = ((0, P),)

        CH = 5
        CHUNKS = EC // CH
        PICK_END = CHUNKS - A.ahead + 1
        jbytes, rbytes = CH * P, CH * 4 * ET
        hotJ = [edge_ring[0:EP, b * (jbytes + rbytes):b * (jbytes + rbytes) + jbytes]
                .rearrange("p (c j) -> p c j", c=CH) for b in range(2)]
        hotR = [edge_ring[0:EP, b * (jbytes + rbytes) + jbytes:(b + 1) * (jbytes + rbytes)]
                .rearrange("p (c f t) -> p c f t", c=CH, f=4) for b in range(2)]
        SG = 3
        assert 2 * SG * R == ET
        diag = [edge_ring[:, b * SG * P:(b + 1) * SG * P].rearrange("p (t j) -> p t j", t=SG) for b in range(2)]
        earlier = edge_ring[:, 2 * SG * P:(2 * SG + 1) * P]
        low_at_word = (2 * SG + 1) * P
        low = [edge_ring[:, low_at_word + b * SG * P // 2:low_at_word + (b + 1) * SG * P // 2].bitcast(F16)
               .rearrange("p (t j) -> p t j", t=SG) for b in range(2)]
        assert low_at_word + SG * P <= MS * WIDE
        DG = 5
        assert 2 * DG * (ET // U - 2) == EC
        diag2 = [d[:, 0:2, :] for d in diag]
        low2 = [d[:, 0:2, :] for d in low]
        free = edge_ring[:, low_at_word + SG * P:MS * WIDE]
        earlier_count = free[:, 0:EC]
        target2 = free[:, EC:2 * EC]
        index2 = free[:, 2 * EC:4 * EC].bitcast(I32).rearrange("p (t n) -> p t n", n=2)
        same2 = gring[:, :, :, :].rearrange("p s g d -> p (s g d)")[:, 0:EC * P // 2].bitcast(F16)\
            .rearrange("p (t j) -> p t j", j=P)
        Bp.set_graph(same, index)
        Dp.set_graph(same, index)
        Fp.set_graph(same2, index2)
        words = CH * P // 2 * 2 + CH * NT // 2
        deg_space = [gring[0:EP, 2 + b, :, :].rearrange("p g d -> p (g d)") for b in range(2)]
        hot16 = [g[:, 0:words].bitcast(F16) for g in deg_space]
        reach = [h[:, 0:CH * P].rearrange("p (c q) -> p c q", c=CH) for h in hot16]
        hotQ = [h[:, CH * P:2 * CH * P].rearrange("p (c q) -> p c q", c=CH) for h in hot16]
        hotT = [h[:, 2 * CH * P:2 * CH * P + CH * NT].rearrange("p (c t) -> p c t", c=CH) for h in hot16]
        node_q = [g[:, words:words + CH] for g in deg_space]
        node_t = [g[:, words + CH:words + 2 * CH] for g in deg_space]
        assert words + 2 * CH <= GT * D and CHUNKS == 2 * (ET // U - 2)
        mask = act[0:EP, 0, 0:R * EC]
        run = act[0:EP, 1, 0:R * EC]
        mask3 = mask.rearrange("p (r c) -> p r c", r=R)
        run3 = run.rearrange("p (r c) -> p r c", r=R)
        term = [[msgs[:, 2 * b + h, 0:D] for h in range(2)] for b in range(2)]
        raw = [gring[:, 2 * n:2 * n + 2, :, :].rearrange("p s g d -> p (s g) d") for n in range(2)]

        scale_at = ({0: 0, 2: 1, 4: 2, 6: 3}, {0: 0, 1: 1, 3: 2, 5: 3})
        sum_at = ({1: 0, 3: 1, 5: 2, 7: 3}, {1: 0, 2: 1, 4: 2, 6: 3})
        round_at = ({1: 0, 3: 1, 5: 2, 7: 3}, {2: 0, 3: 1, 5: 2, 7: 3})
        low_at = ({1: 0, 3: 1, 5: 2, 7: 3}, {2: 0, 4: 1, 6: 2, 7: 3})

        block = ctx.enter_context(nc.Block())

        @block.sync
        def _(sp):
            for n, a in enumerate((src, dst, etype)):
                sp.dma_start(edge_i[0:EP, n, :], a.rearrange("(p c) -> p c", c=EC)).then_inc(edges_in, 16)
            sp.dma_start(edge_w[0:EP, :], weight.rearrange("(p c) -> p c", c=EC)).then_inc(edges_in, 16)
            sp.dma_start(raw[0], loop0.rearrange("(c p) d -> p c d", p=P)).then_inc(loops_in[0], 16)
            for n, a in enumerate((comp0, comp1)):
                sp.dma_start(comp[n][:, :], a.rearrange("(o r) b -> o (r b)", o=1).to_broadcast([P, R * B]))\
                  .then_inc(consts_in, 16)
            for n, a in enumerate((bias0, bias1, bias2)):
                sp.dma_start(bias[n][:, :], a.rearrange("(o d) -> o d", o=1).to_broadcast([P, D]))\
                  .then_inc(consts_in, 16)

            def load(ring, arrived, parts, table, width, i, s):
                for a, b in parts:
                    source = table[a:b, bass.ds((i * len(ring) + s) * (GT * width), GT * width)]
                    sp.dma_start(ring[s][a:b, :, 0:width], source.rearrange("p (g d) -> p g d", g=GT))\
                      .then_inc(arrived[s], 16)

            def store(pp, parts, table, width, i, s):
                n = s % len(pp.results)
                for a, b in parts:
                    target = table[a:b, bass.ds((i * len(pp.x) + s) * (GT * width), GT * width)]
                    sp.dma_start(target.rearrange("p (g d) -> p g d", g=GT), pp.results[n][a:b, :, 0:width])\
                      .then_inc(pp.stored[n], 16)

            def hold(condition, value):
                sp.wait_ge(condition, value)
                if not isinstance(value, int):
                    sp.sem_inc(sp_turn, 1)

            def node_pass(pp, load_group, release, store_group, done, near_end=lambda: None):
                slots = len(pp.x)
                last = NT // GT // slots - 1

                def turn(i, s, more):
                    if more:
                        release(i * slots + s)
                        load_group(i + 1, s)
                    done(i * slots + s)
                    store_group(i, s)

                with sp.Fori(0, last) as i:
                    for s in range(slots):
                        turn(i, s, True)
                near_end()
                for s in range(slots):
                    turn(last, s, False)

            def store_a(i, s):
                store(A, WHOLE, acc1_nodes, D, i, s)
                target = acc3_nodes[:, bass.ds((i * XS + s) * (GT * D), GT * D)]
                sp.dma_start(target.rearrange("p (g d) -> p g d", g=GT),
                             zeros[:, 0:D].unsqueeze(1).to_broadcast([P, GT, D])).then_inc(tables_zeroed, 16)

            def load_a(i, s):
                load(A.x, A.x_in, PARTS, x_nodes, D, i, s)

            def load_third_matrix():
                sp.wait_ge(split_lo, 1 + KC)
                sp.dma_start(raw[0], w2t.rearrange("(c p) d -> p c d", p=P)).then_inc(loops_in[2], 16)

            sp.wait_ge(cleared, 1)
            sp.wait_ge(ring_cleared, 1)
            for s in range(XS):
                load_a(0, s)
            sp.dma_start(raw[1], loop1.rearrange("(c p) d -> p c d", p=P)).then_inc(loops_in[1], 16)
            for b in range(B):
                sp.dma_start(basis[:, b, :, :], basis0[b].rearrange("(c p) d -> p c d", p=P))\
                  .then_inc(basis_in[0], 16)
            node_pass(A, load_a,
                      lambda q: hold(normed, A.norm0 + GT * q + GT),
                      store_a,
                      lambda q: hold(evac_v, A.evac0 + GT * q + GT),
                      near_end=load_third_matrix)

            sp.wait_ge(rel_free, BLOCKS + 2)
            with sp.Fori(0, B) as b:
                for c in range(KC):
                    hold(index_put, KC * b + c + LEAD + 2)
                    sp.dma_start(basis[:, bass.ds(b, 1), c, :],
                                 basis1[bass.ds(b, 1), c * P:(c + 1) * P, :].rearrange("b p d -> p b d"))\
                      .then_inc(basis_in[1], 16)

            def load_c_table(i, s):
                load(C.x, C.x_in, WHOLE, acc1_nodes, D, i, s)

            def load_c_other(i, s):
                load(C.other, C.other_in, PARTS, x_nodes, D, i, s)

            def load_c(i, s):
                load_c_table(i, s)
                load_c_other(i, s)

            sp.wait_ge(split_lo, 1 + 2 * KC)
            for s in range(XS):
                if s == XS // 2:
                    sp.wait_ge(graph_ready, 3)
                load_c_other(0, s)
            sp.wait_ge(added, 16 * ET)
            for s in range(XS):
                load_c_table(0, s)
            sp.wait_ge(cleared, 2)

            def done_c(q):
                hold(dis_put, q + 1)
                hold(evac_v, C.evac0 + GT * q + GT)

            def release_c(q):
                hold(turned, C.tile0 + GT * q + GT)
                hold(evac_v, C.evac0 + GT * q + GT)

            node_pass(C, load_c, release_c, lambda i, s: store(C, WHOLE, acc2_nodes, WIDE, i, s), done_c)

            def load_z_table(i, s):
                load(Z.x, Z.x_in, WHOLE, acc2_nodes, WIDE, i, s)

            def load_z_other(i, s):
                load(Z.other, Z.other_in, WHOLE, acc3_nodes, D, i, s)

            def load_z(i, s):
                load_z_table(i, s)
                load_z_other(i, s)

            sp.wait_ge(added, 16 * 2 * ET)
            for s in range(len(Z.x)):
                sp.wait_ge(index_put, 2 * ET + LEAD + 6 + 3 * s)
                load_z_table(0, s)
            sp.wait_ge(added, 16 * (2 * ET + EC))
            for s in range(len(Z.x)):
                load_z_other(0, s)

            def done_z(q):
                hold(finished, GT * q + GT)

            node_pass(Z, load_z, done_z, lambda i, s: store(Z, PARTS, out_nodes, D, i, s), done_z)
            sp.wait_ge(tables_zeroed, 16 * NT // GT)
            for s in range(OS):
                sp.wait_ge(stored[s], 16 * (NT // GT // OS) * 2)
            for s in range(len(Z.results)):
                sp.wait_ge(z_stored[s], 32 * (NT // GT // len(Z.results)))

        @block.gpsimd
        def _(pool):
            pool.memset(zeros[:, :], 0.0).then_inc(cleared, 1)
            pool.memset(oring[:, :, :, D:WIDE], 0.0).then_inc(cleared, 1)
            pool.iota(iota_i[:, :], pattern=[[1, P]], base=0, channel_multiplier=0).then_inc(pool_const, 1)
            pool.iota(spare_i[:, :], pattern=[[1, 1]], base=N, channel_multiplier=1).then_inc(pool_const, 1)
            pool.memset(ones[:, :], 1.0).then_inc(pool_const, 1)
            pool.memset(ident[:, :], 0.0).then_inc(pool_const, 1)
            pool.wait_ge(pool_const, 4)
            pool.affine_select(out=ident[:, :], in_=ident[:, :], compare_op=ALU.not_equal, fill=1.0,
                               base=0, pattern=[[-1, P]], channel_multiplier=1).then_inc(pool_const, 1)
            pool.affine_select(out=before[:, :], in_=ones[:, :], compare_op=ALU.is_gt, fill=0.0,
                               base=0, pattern=[[1, P]], channel_multiplier=-1).then_inc(pool_const, 1)
            pool.wait_ge(recorded, 1)
            pool.affine_select(out=earlier, in_=ones[:, :], compare_op=ALU.is_gt, fill=0.0,
                               base=0, pattern=[[-1, P]], channel_multiplier=1).then_inc(pool_const, 1)
            pool.wait_ge(pool_const, 7)

            def hold(condition, value):
                pool.wait_ge(condition, value)
                if not isinstance(value, int):
                    pool.sem_inc(pool_turn, 1)

            def edge_steps(ep, table, width, sums, sum_width, ready):
                def step(i, k):
                    g = i * U + k + LEAD
                    if inside(g, ep.tiles):
                        s = (k + LEAD) % GS
                        if ep is Dp and isinstance(g, int) and g < GS:
                            pool.wait_ge(turned, C.tile0 + NT - GS + g + 1)
                        else:
                            hold(normed, ep.norm0 + g - GS + 1)
                        if ep is Fp and (not isinstance(g, int) or g >= GS):
                            hold(rows_lo, ep.number * ET + g - GS + 1)
                            hold(mixed, g - GS + 1)
                        pool.tensor_copy(index_now[:, (k + LEAD) % U, 0:1], ep.index[:, bass.ds(g, 1), 0])\
                            .then_inc(index_put, 1)
                        hold(index_put, ep.number * ET + g + 1)
                        pool.indirect_dma_start(
                            rows[:, s, 0:width], None, table,
                            bass.IndirectOffsetOnAxis(ap=index_now[:, (k + LEAD) % U, 0:1], axis=0))\
                            .then_inc(gathered[s], 16)
                    t = i * U + k
                    if inside(t + 1, ep.tiles) and (not isinstance(t, int) or t >= -1):
                        pool.tensor_copy(index_now[:, (k + 1) % U, 1:2], ep.index[:, bass.ds(t + 1, 1), 1])\
                            .then_inc(target_put, 1)
                    if inside(t, ep.tiles):
                        hold(target_put, ep.number * ET + t + 1)
                        if ep is Fp:
                            hold(evac_v, ep.evac0 + t + 1)
                        else:
                            hold(evac_s, ep.evac0 + t + 1)
                        if isinstance(t, int) and t == 0:
                            ready()
                        else:
                            hold(added, 16 * (ep.number * ET + t))
                        pool.indirect_dma_start(
                            sums, bass.IndirectOffsetOnAxis(ap=index_now[:, k % U, 1:2], axis=0),
                            msgs[:, k % MS, 0:sum_width], None, compute_op=ALU.add).then_inc(added, 16)

                return step

            pool.sem_inc(rel_summed, 2)
            pool.sem_inc(rel_free, 2)

            def combine(layer, i, k):
                at = (i - 1) * (2 * KC * D)
                if k in sum_at[layer]:
                    kc = sum_at[layer][k]
                    n = BLOCKS * layer + (i - 1) * KC + kc
                    hold(bases_added, 2 * n + 2)
                    hold(rel_free, n + 1)
                    pool.tensor_tensor(combined[:, kc % 2, :], term[kc % 2][0], term[kc % 2][1], ALU.add)\
                        .then_inc(rel_summed, 1)
                if k in low_at[layer]:
                    kc = low_at[layer][k]
                    n = BLOCKS * layer + (i - 1) * KC + kc
                    hold(rel_high, n + 1)
                    pool.tensor_tensor(rel_w[:, bass.ds(at + (KC + kc) * D, D)], combined[:, kc % 2, :],
                                       rel_w[:, bass.ds(at + kc * D, D)], ALU.subtract).then_inc(rel_free, 1)

            def compare(i, k):
                if k in (3, 6):
                    h = (k - 3) // 3
                    n = 2 * (i - 1) + h
                    hold(same_done, n + 1)
                    pool.tensor_tensor(low[h], same[:, bass.ds(SG * n, SG), :],
                                       earlier.unsqueeze(1).to_broadcast([P, SG, P]), ALU.mult)\
                        .then_inc(lower_done, 1)
                if k in (0, 3):
                    h = k // 3
                    dst = rec[:, 1, bass.ds(SG * (2 * (i - 1) + h), SG)].unsqueeze(2).to_broadcast([P, SG, P])
                    pool.tensor_tensor(diag[h], ident[:, :].unsqueeze(1).to_broadcast([P, SG, P]), dst, ALU.mult)\
                        .then_inc(spread, 1)

            with pool.Fori(1, R + 1) as i:
                for k in range(U):
                    compare(i, k)
                    combine(0, i, k)

            pool.wait_ge(graph_ready, 2)

            def ready_b():
                for s in range(OS):
                    pool.wait_ge(stored[s], 16 * (NT // GT // OS))

            steps(pool, ET, U, LEAD, edge_steps(Bp, x, D, acc1, D, ready_b))

            def step_c(i, k):
                a = i * U + k + 2
                if k % GT == 0 and inside(a, NT):
                    q = (k + 2) % U // GT
                    hold(C.other_in[q], 32 * (i + (k + 2) // U + 1))
                    pool.tensor_tensor(gring[:, q, :, :], gring[:, q, :, :],
                                       bias[1][:, :].unsqueeze(1).to_broadcast([P, GT, D]), ALU.add)\
                        .then_inc(g_biased, 1)
                if not isinstance(i, int):
                    combine(1, i, k)
                if k % GT == 1 and k > 0:
                    q = k // GT
                    hold(stored[q % OS], 16 * (NT // GT // OS + i * (XS // OS) + q // OS))
                    pool.tensor_copy(oring[:, q % OS, :, D:D + 1],
                                     dis[:, bass.ds((i * XS + q) * GT, GT)].unsqueeze(2)).then_inc(dis_put, 1)

            def ready_d():
                pool.wait_ge(message_ends, 1)
                for s in range(OS):
                    pool.wait_ge(stored[s], 16 * 2 * (NT // GT // OS))

            pool.wait_ge(graph_ready, 3)
            pool.wait_ge(added, 16 * ET)
            step_d = edge_steps(Dp, acc1, D, acc2, WIDE, ready_d)
            steps(pool, NT, U, 2, step_c, after_last=ahead_of(step_d, LEAD))

            steps(pool, ET, U, 0, step_d)

            pool.wait_ge(added, 16 * 2 * ET)
            pool.wait_ge(graph_ready, 4)
            steps(pool, EC, U, LEAD, edge_steps(Fp, acc2, WIDE, acc3, D,
                                                lambda: pool.wait_ge(tables_zeroed, 16 * NT // GT)))

            def step_z(i, k):
                t = i * Z.unroll + k
                if inside(t - 2, NT):
                    q, j = (k - 2) % Z.unroll // GT, k % GT
                    if j == 0:
                        hold(Z.other_in[q], 16 * (i + (k - 2) // Z.unroll + 1))
                    hold(evac_v, Z.evac0 + t - 1)
                    o = Z.results[q][:, j, 0:D]
                    pool.tensor_tensor(o, o, Z.other[q][:, j, :], ALU.add).then_inc(third_added, 1)
                for f in lags(i, k, FINISH, 3):
                    if inside(t - f, NT):
                        q, j = (k - f) % Z.unroll // GT, (k - f) % GT
                        hold(rectified, t - f + 1)
                        o = Z.results[q][:, j, 0:D]
                        pool.tensor_tensor(o, o, Z.x[q][:, j, 0:D], ALU.add).then_inc(finished, 1)

            steps(pool, NT, Z.unroll, 0, step_z, tail=3)

        @block.scalar
        def _(sc):
            def split_high_of_matrix(n, chunks, done_with):
                sc.wait_ge(loops_in[n], 16)
                wait(sc, product, done_with)
                sc.activation(node_w[n % 2][:, 0, chunks, :], raw[n % 2][:, chunks, :], ACT.Copy, scale=SCALE)\
                  .then_inc(split_hi, 1)

            sc.wait_ge(cleared, 1)
            ring_rows = xring[96:P, :, :, :].rearrange("p s g d -> p (s g d)")
            sc.activation(ring_rows, zeros[96:P, 0:1].to_broadcast([P - 96, XS * GT * WIDE]), ACT.Copy)\
              .then_inc(ring_cleared, 1)
            split_high_of_matrix(0, slice(0, KC), 0)

            def std_unit(pp, n, col, width):
                per = width
                sc.wait_ge(moment, pp.ln0 + per * n + per)
                sc.activation(std[:, col:col + width], moments[:, col:col + width, 1], ACT.Sqrt,
                              bias=eps[:, 0:1]).then_inc(deviation, 1)

            def split_high(pp, t, k):
                sc.wait_ge(turned, pp.tile0 + t + 1)
                wait(sc, product, pp.tile0 + t - 1)
                sc.activation(actT[:, k % 2, 0, :], psT[:, k % 2, :], ACT.Relu if pp is C else ACT.Copy)\
                  .then_inc(hi_done, 1)

            def hold(condition, value):
                sc.wait_ge(condition, value)
                sc.sem_inc(act_turn, 1)

            def scale_bases(layer, i, kc):
                n = BLOCKS * layer + (i - 1) * KC + kc
                if kc == 0:
                    sc.wait_ge(basis_in[layer], 16 * B * (KC if layer else 1))
                hold(rel_summed, n + 1)
                for h in range(2):
                    sc.activation(term[kc % 2][h], basis[:, 2 * h, kc, :], ACT.Copy,
                                  scale=comp[layer][:, bass.ds((i - 1) * B + 2 * h, 1)]).then_inc(bases_scaled, 1)

            def round_block(layer, i, kc):
                n = BLOCKS * layer + (i - 1) * KC + kc
                hold(rel_summed, n + 3)
                sc.activation(rel_w[:, bass.ds((i - 1) * (2 * KC * D) + kc * D, D)], combined[:, kc % 2, :], ACT.Copy)\
                  .then_inc(rel_high, 1)

            def node_step(pp, i, k):
                t = i * pp.unroll + k
                if inside(t + 1, NT):
                    split_high(pp, t + 1, k + 1)
                a = t + 2
                if pp.ln0 is not None and inside(a, NT):
                    c = (k + 2) % U
                    q, j = (k + 2) % pp.unroll // GT, k % GT
                    if j == 0:
                        sc.wait_ge(shift, pp.unit0 + i * (pp.unroll // GT) + (k + 2) // GT + 1)
                    wait(sc, turned, pp.tile0 + a - 1)
                    sc.activation(act[:, c % 2, :], pp.x[q][:, j, 0:D], ACT.Relu,
                                  scale=rstd[:, c:c + 1], bias=nmean[:, c:c + 1]).then_inc(normed, 1)
                    if pp is Z:
                        if not isinstance(a, int) or a >= 4:
                            sc.wait_ge(evac_v, Z.evac0 + a - 3)
                        sc.activation(scaled_bias[:, c % 4, :], bias[2][:, :], ACT.Copy,
                                      scale=pp.x[q][:, j, D:D + 1]).then_inc(bias_scaled, 1)
                for r in lags(i, k, FINISH - 1, 2) if pp is Z else []:
                    if inside(t - r, NT):
                        q, j = (k - r) % pp.unroll // GT, (k - r) % GT
                        sc.wait_ge(third_added, t - r + 1)
                        o = pp.results[q][:, j, 0:D]
                        sc.activation(o, o, ACT.Relu, scale=pp.x[q][:, j, D:D + 1]).then_inc(rectified, 1)
                if pp is A and isinstance(i, int) and i == 0 and 0 <= k - (U - KC) + 1 < KC:
                    split_high_of_matrix(1, slice(k - (U - KC) + 1, k - (U - KC) + 2), 0)
                e = k + pp.ahead - 1
                if pp.ln0 is not None and k % GT == 1 and inside(t + pp.ahead - 1, NT):
                    std_unit(pp, i * (pp.unroll // GT) + e // GT, e % U, GT)
                if pp is not Z and not isinstance(i, int):
                    layer = pp.number
                    if k in round_at[layer]:
                        round_block(layer, i, round_at[layer][k])
                    if k in scale_at[layer]:
                        scale_bases(layer, i, scale_at[layer][k])

            def edge_step(ep, i, k):
                h = i * U + k + 1
                if inside(h, ep.tiles):
                    split_high(ep, h, k + 1)
                if ep is Fp and inside(h, ep.tiles):
                    if not isinstance(h, int) or h >= 2:
                        sc.wait_ge(bias_row, h - 1)
                    sc.activation(weight_sum[:, (k + 1) % 2:(k + 1) % 2 + 1], psS[:, (k + 1) % 2, 0:1], ACT.Copy)\
                      .then_inc(summed, 1)
                held = hold if not isinstance(i, int) else sc.wait_ge
                b = i * U + k + 2
                if inside(b, ep.tiles):
                    c = k % 2
                    if isinstance(b, int) and b < 2 and ep is not Fp:
                        sc.wait_ge(rel_free, (ep.number + 1) * BLOCKS + 2)
                    held(turned, ep.tile0 + b - 1)
                    held(normed, ep.norm0 + b + 1)
                    weight = rows[:, (k + 2) % GS, D:D + 1] if ep is Fp else rec[:, 2, bass.ds(b, 1)]
                    sc.activation(parted[:, c, 0, :], act[:, c, :], ACT.Copy, scale=weight).then_inc(rows_hi, 1)
                n = i * U + k + 3
                if inside(n, ep.tiles):
                    c = (k + 3) % U
                    s = c % GS
                    if isinstance(n, int) and n < 2 and ep is Bp:
                        sc.wait_ge(turned, ep.tile0 + n - 1)
                    else:
                        sc.wait_ge(rows_lo, ep.number * ET + n - 1)
                    if ep.ln0 is not None:
                        sc.wait_ge(shift, ep.unit0 + n + 1)
                        sc.activation(act[:, c % 2, :], rows[:, s, 0:D], ACT.Relu,
                                      scale=rstd[:, c:c + 1], bias=nmean[:, c:c + 1]).then_inc(normed, 1)
                    else:
                        sc.wait_ge(gathered[s], 16 * (ep.number * (ET // GS) + i * (U // GS) + (k + 3) // GS + 1))
                        sc.activation(act[:, c % 2, :], rows[:, s, 0:D], ACT.Relu).then_inc(normed, 1)
                a = i * U + k + 4
                if ep.ln0 is not None and inside(a, ep.tiles):
                    std_unit(ep, a, (k + 4) % U, 1)
                if ep is Fp and inside(h, ep.tiles):
                    if not isinstance(h, int) or h >= 4:
                        sc.wait_ge(evac_v, ep.evac0 + h - 3)
                    held(summed, h + 1)
                    sc.activation(bias_rows[:, (k + 1) % 4, :], bias[2][:, :], ACT.Copy,
                                  scale=weight_sum[:, (k + 1) % 2:(k + 1) % 2 + 1]).then_inc(bias_row, 1)
                if ep is Bp and isinstance(i, int) and i == 0 and 0 <= k < KC:
                    split_high_of_matrix(2, slice(k, k + 1), A.tile0 + NT)
                if ep is Bp and isinstance(i, int) and i > 0 and k == 1:
                    sc.wait_ge(deg_added, 1 + CHUNKS)
                    sc.activation(dis[:, :], dis[:, :], ACT.Sqrt).then_inc(deg_std, 1)
                t = i * U + k - 1
                if ep is not Fp and inside(t, ep.tiles):
                    sc.wait_ge(product, ep.tile0 + t + 1)
                    wait(sc, added, 16 * (ep.number * ET + t - MS + 1))
                    sc.activation(msgs[:, (k - 1) % MS, 0:D], psZ[:, (k - 1) % ZS, :], ACT.Copy, scale=1.0 / SCALE)\
                      .then_inc(evac_s, 1)

            sc.wait_ge(comp_scaled, 2)
            step_a, step_b, step_c, step_d, step_f, step_z = (
                lambda i, k, step=step, pp=pp: step(pp, i, k)
                for step, pp in ((node_step, A), (edge_step, Bp), (node_step, C), (edge_step, Dp),
                                 (edge_step, Fp), (node_step, Z)))
            steps(sc, NT, U, A.ahead, step_a, after_last=ahead_of(step_b, 4))
            steps(sc, ET, U, 0, step_b, tail=1)
            sc.wait_ge(added, 16 * ET)
            steps(sc, NT, U, 1, step_c, after_last=ahead_of(step_d, 4))
            steps(sc, ET, U, 0, step_d, tail=1)
            steps(sc, EC, U, 4, step_f, after_last=ahead_of(step_z, Z.ahead, Z.ahead - 4))
            steps(sc, NT, Z.unroll, 0, step_z, tail=2)

        @block.vector
        def _(v):
            done = [0]

            def link(ins):
                done[0] += 1
                ins.then_inc(setup, 1)
                v.wait_ge(setup, done[0])

            link(v.memset(eps[:, :], EPS))
            v.memset(dis[:, :], 1.0).then_inc(deg_added, 1)
            v.wait_ge(pool_const, 6)
            v.tensor_copy(iota[:, :], iota_i[:, :]).then_inc(setup, 1)
            done[0] += 1
            link(v.tensor_copy(spare[:, :], spare_i[:, :]))
            link(v.tensor_scalar(iota_nt[:, :], iota[:, :], float(NT), None, ALU.mult))
            link(v.tensor_scalar(iota1[:, :], iota[:, :], 1.0, None, ALU.add))

            def split_low_of_matrix(n, chunks, halves_done):
                v.wait_ge(split_hi, halves_done)
                m = n % 2
                v.scalar_tensor_tensor(out=node_w[m][:, 1, chunks, :].rearrange("p c d -> p (c d)"),
                                       in0=raw[m][:, chunks, :].rearrange("p c d -> p (c d)"), scalar=SCALE,
                                       in1=node_w[m][:, 0, chunks, :].rearrange("p c d -> p (c d)"),
                                       op0=ALU.mult, op1=ALU.subtract).then_inc(split_lo, 1)

            link(v.memset(edge_f[:, :, :], 0.0))
            v.wait_ge(edges_in, 64)
            link(v.tensor_copy(edge_f[0:EP, :, :], edge_i[0:EP, :, :]))
            link(v.tensor_tensor(mask3, edge_f[0:EP, 2, :].unsqueeze(1).to_broadcast([EP, R, EC]),
                                 iota[0:EP, 0:R].unsqueeze(2).to_broadcast([EP, R, EC]), ALU.is_equal))
            link(v.tensor_tensor_scan(run, ones[0:EP, 0:1].to_broadcast([EP, R * EC]), mask, 0.0,
                                      ALU.mult, ALU.add))
            link(v.tensor_copy(counts[0:EP, 0, :], run3[:, :, EC - 1]))
            link(v.tensor_tensor(run3[:, 1:R, :], run3[:, 1:R, :],
                                 counts[0:EP, 0, 0:R - 1].unsqueeze(2).to_broadcast([EP, R - 1, EC]), ALU.subtract))
            link(v.tensor_copy(counts[0:EP, 1, :], run3[:, :, EC - 1]))
            counted_here = done[0]
            v.wait_ge(setup_pe, 1)
            link(v.tensor_scalar(counts_i[:, :], psZ[:, 1, 0:R], float(P - 1), None, ALU.add))
            link(v.tensor_scalar(counts_i[:, :], counts_i[:, :], 7, None, ALU.arith_shift_right))
            link(v.tensor_copy(counts[:, 2, :], counts_i[:, :]))
            link(v.tensor_tensor_scan(counts[:, 3, :], ones[:, 0:R], counts[:, 2, :], 0.0, ALU.mult, ALU.add))
            link(v.tensor_tensor(counts[:, 4, :], counts[:, 3, :], counts[:, 2, :], ALU.subtract))
            link(v.scalar_tensor_tensor(out=counts[:, 5, :], in0=counts[:, 4, :], scalar=float(P),
                                        in1=psZ[:, 0, 0:R], op0=ALU.mult, op1=ALU.add))
            link(v.tensor_tensor(run3, run3, counts[0:EP, 5, :].unsqueeze(2).to_broadcast([EP, R, EC]), ALU.add))
            link(v.tensor_tensor(mask3, mask3, run3, ALU.mult))
            link(v.tensor_reduce(place[0:EP, 0, :], mask3.rearrange("p r c -> p c r"), AX_X, ALU.add))
            link(v.tensor_scalar(place_i[0:EP, 0, :], place[0:EP, 0, :], -1.0, None, ALU.add))
            link(v.tensor_scalar(place_i[0:EP, 1, :], place_i[0:EP, 0, :], 7, None, ALU.arith_shift_right))
            link(v.tensor_scalar(place_i[0:EP, 2, :], place_i[0:EP, 0, :], P - 1, None, ALU.bitwise_and))
            v.tensor_copy(place[0:EP, 1:3, :], place_i[0:EP, 1:3, :]).then_inc(placed, 1)
            link(v.tensor_copy(edge_f[0:EP, 2, :], edge_w[0:EP, :]))

            last_rel = act[:, 0, 0:ET * R].rearrange("p (t r) -> p t r", t=ET)
            link(v.tensor_tensor(last_rel, counts[:, 3, :].unsqueeze(1).to_broadcast([P, ET, R]),
                                 iota[:, 0:ET].unsqueeze(2).to_broadcast([P, ET, R]), ALU.is_le))
            link(v.tensor_reduce(flag[:, 0, :], last_rel, AX_X, ALU.add))
            v.tensor_scalar(tile_rel[:, :], flag[:, 0, :], float(R - 1), None, ALU.min).then_inc(graph_ready, 1)

            split_low_of_matrix(0, slice(0, KC), 1)
            v.wait_ge(placed, 1)

            def pick(n):
                wait(v, picked_used, n - 1)
                v.tensor_tensor(hotR[n % 2][:, :, 3, :], iota[0:EP, 0:ET].unsqueeze(1).to_broadcast([EP, CH, ET]),
                                place[0:EP, 1, n * CH:(n + 1) * CH].unsqueeze(2).to_broadcast([EP, CH, ET]),
                                ALU.is_equal).then_inc(picked, 1)
                v.tensor_tensor(hotJ[n % 2], iota[0:EP, :].unsqueeze(1).to_broadcast([EP, CH, P]),
                                place[0:EP, 2, n * CH:(n + 1) * CH].unsqueeze(2).to_broadcast([EP, CH, P]),
                                ALU.is_equal).then_inc(picked, 1)
                v.wait_ge(picked, 3 * n + 1)
                values = edge_f[0:EP, :, n * CH:(n + 1) * CH].rearrange("p f c -> p c f")
                v.tensor_tensor(hotR[n % 2][:, :, 0:3, :],
                                hotR[n % 2][:, :, 3, :].unsqueeze(2).to_broadcast([EP, CH, 3, ET]),
                                values.unsqueeze(3).to_broadcast([EP, CH, 3, ET]), ALU.mult).then_inc(picked, 1)

            def take_records():
                v.wait_ge(picked_used, CHUNKS)
                link(v.tensor_copy(rec[:, :, :].rearrange("p f t -> p (f t)"), psS[:, 0, 0:4 * ET]))
                link(v.tensor_scalar(flag[:, 0, :], rec[:, 3, :], -1.0, 1.0, ALU.mult, ALU.add))
                v.scalar_tensor_tensor(out=rec[:, 1, :], in0=flag[:, 0, :], scalar=spare[:, 0:1],
                                       in1=rec[:, 1, :], op0=ALU.mult, op1=ALU.add).then_inc(recorded, 1)
                link(v.tensor_copy(index[:, :, 0], rec[:, 0, :]))
                link(v.tensor_scalar(flag[:, 0, 0:1], spare[:, 0:1], N + EP - 0.5, None, ALU.is_gt))
                link(v.tensor_tensor(flag[:, 0, 0:1], flag[:, 0, 0:1], spare[:, 0:1], ALU.mult))
                link(v.tensor_scalar(edge_f[:, 1, :], edge_f[:, 1, :], flag[:, 0, 0:1], None, ALU.add))

            def compare(i, k):
                if k in (2, 5):
                    h = (k - 2) // 3
                    n = 2 * (i - 1) + h
                    v.wait_ge(spread_pe, n + 1)
                    v.tensor_tensor(same[:, bass.ds(SG * n, SG), :],
                                    psS[:, h, 0:SG * P].rearrange("p (t j) -> p t j", t=SG),
                                    rec[:, 1, bass.ds(SG * n, SG)].unsqueeze(2).to_broadcast([P, SG, P]),
                                    ALU.is_equal).then_inc(same_done, 1)
                if k in (4, 7):
                    h = (k - 4) // 3
                    n = 2 * (i - 1) + h
                    v.wait_ge(lower_done, n + 1)
                    v.sem_inc(dve_turn, 1)
                    v.tensor_reduce(flag[:, 1, bass.ds(SG * n, SG)], low[h], AX_X, ALU.add).then_inc(counted, 1)

            def targets(earlier_of, scratch, dst, to):
                link(v.tensor_scalar(earlier_of, earlier_of, 0.5, None, ALU.is_gt))
                link(v.tensor_scalar(scratch, dst, spare[:, 0:1], None, ALU.subtract))
                link(v.tensor_tensor(scratch, scratch, earlier_of, ALU.mult))
                link(v.tensor_tensor(scratch, dst, scratch, ALU.subtract))
                v.tensor_copy(to, scratch).then_inc(graph_ready, 1)

            def compare_dense(i, k):
                for j in range(DG):
                    n = DG * (i - 1) + j
                    dst = edge_f[:, 1, bass.ds(2 * n, 2)].unsqueeze(2).to_broadcast([P, 2, P])
                    if k == j + 2:
                        v.wait_ge(dense_pe, n + 1)
                        v.tensor_tensor(same2[:, bass.ds(2 * n, 2), :],
                                        psS[:, j % 2, 0:2 * P].rearrange("p (t j) -> p t j", t=2), dst,
                                        ALU.is_equal).then_inc(dense_same, 1)
                for j in range(DG):
                    n = DG * (i - 1) + j
                    dst = edge_f[:, 1, bass.ds(2 * n, 2)].unsqueeze(2).to_broadcast([P, 2, P])
                    if k == j + 3:
                        v.wait_ge(dense_same, n + 1)
                        v.wait_ge(dense_counted, n + 1)
                        v.tensor_tensor(low2[j % 2], same2[:, bass.ds(2 * n, 2), :],
                                        earlier.unsqueeze(1).to_broadcast([P, 2, P]), ALU.mult)\
                         .then_inc(dense_low, 1)
                    if k == j:
                        v.tensor_tensor(diag2[j % 2], ident[:, :].unsqueeze(1).to_broadcast([P, 2, P]), dst, ALU.mult)\
                         .then_inc(dense_diag, 1)
                for j in range(DG):
                    n = DG * (i - 1) + j
                    if k == j + 3:
                        v.wait_ge(dense_low, n + 1)
                        v.sem_inc(dve_turn, 1)
                        v.tensor_reduce(earlier_count[:, bass.ds(2 * n, 2)], low2[j % 2], AX_X, ALU.add)\
                         .then_inc(dense_counted, 1)

            def count_degrees(i, k):
                for h, first in ((0, 0), (1, 3)):
                    n = 2 * (i - 1) + h
                    base = 6 * n
                    nodes = edge_f[0:EP, 0, bass.ds(CH * n, CH)]
                    part = k - first
                    if part == 0:
                        v.tensor_tensor(reach[h], iota_nt[0:EP, :].unsqueeze(1).to_broadcast([EP, CH, P]),
                                        nodes.unsqueeze(2).to_broadcast([EP, CH, P]), ALU.is_le).then_inc(deg_hot, 1)
                    if part == 1:
                        v.wait_ge(deg_hot, base + 1)
                        v.sem_inc(dve_turn, 1)
                        v.tensor_reduce(node_q[h], reach[h], AX_X, ALU.add).then_inc(deg_hot, 1)
                    if part == 2:
                        v.wait_ge(deg_hot, base + 2)
                        v.tensor_scalar(node_t[h], node_q[h], -float(NT), float(NT), ALU.mult, ALU.add)\
                         .then_inc(deg_hot, 1)
                        v.wait_ge(deg_hot, base + 3)
                        v.tensor_tensor(node_t[h], node_t[h], nodes, ALU.add).then_inc(deg_hot, 1)
                        v.wait_ge(deg_hot, base + 4)
                        v.tensor_tensor(hotT[h], iota[0:EP, 0:NT].unsqueeze(1).to_broadcast([EP, CH, NT]),
                                        node_t[h].unsqueeze(2).to_broadcast([EP, CH, NT]),
                                        ALU.is_equal).then_inc(deg_hot, 1)
                    if part == 3:
                        v.tensor_tensor(hotQ[h], iota1[0:EP, :].unsqueeze(1).to_broadcast([EP, CH, P]),
                                        node_q[h].unsqueeze(2).to_broadcast([EP, CH, P]),
                                        ALU.is_equal).then_inc(deg_hot, 1)
                    if k == (5, 7)[h]:
                        v.wait_ge(deg_used, n + 1)
                        v.wait_ge(deg_added, n + 1)
                        v.tensor_tensor(dis[:, :], dis[:, :], psS[:, h, 0:NT], ALU.add).then_inc(deg_added, 1)

            v.wait_ge(consts_in, 80)
            for n in range(2):
                v.tensor_scalar(comp[n][:, :], comp[n][:, :], SCALE, None, ALU.mult).then_inc(comp_scaled, 1)
            v.wait_ge(comp_scaled, 2)

            def add_bases(layer, i, kc):
                n = BLOCKS * layer + (i - 1) * KC + kc
                for h in range(2):
                    v.wait_ge(bases_scaled, 2 * n + h + 1)
                    v.scalar_tensor_tensor(out=term[kc % 2][h], in0=basis[:, 2 * h + 1, kc, :],
                                           scalar=comp[layer][:, bass.ds((i - 1) * B + 2 * h + 1, 1)],
                                           in1=term[kc % 2][h], op0=ALU.mult, op1=ALU.add).then_inc(bases_added, 1)

            def tile_moments(pp, t, c):
                v.wait_ge(stat, pp.ln0 + t + 1)
                if not isinstance(t, int):
                    v.sem_inc(dve_turn, 1)
                v.bn_aggr(moments[:, c, :], stats[:, c, :]).then_inc(moment, 1)

            def scale_of(pp, unit, c, w):
                v.wait_ge(deviation, pp.unit0 + unit + 1)
                v.reciprocal(rstd[:, c:c + w], std[:, c:c + w]).then_inc(inverse, 1)

            def shift_of(pp, unit, c, w, degrees=None):
                v.wait_ge(inverse, pp.unit0 + unit + 1)
                if degrees is not None:
                    v.tensor_tensor(rstd[:, c:c + w], rstd[:, c:c + w], degrees, ALU.mult).then_inc(inverse_d, 1)
                    v.wait_ge(inverse_d, unit + 1)
                v.scalar_tensor_tensor(out=nmean[:, c:c + w], in0=moments[:, c:c + w, 0], scalar=-1.0,
                                       in1=rstd[:, c:c + w], op0=ALU.mult, op1=ALU.mult).then_inc(shift, 1)

            def split_lower(pp, t, k):
                v.wait_ge(hi_done, pp.tile0 + t + 1)
                s = k % 2
                if pp is C:
                    ins = v.scalar_tensor_tensor(out=actT[:, s, 1, :], in0=psT[:, s, :], scalar=0.0,
                                                 in1=actT[:, s, 0, :], op0=ALU.max, op1=ALU.subtract)
                else:
                    ins = v.tensor_tensor(actT[:, s, 1, :], psT[:, s, :], actT[:, s, 0, :], ALU.subtract)
                ins.then_inc(lo_done, 1)

            def node_step(pp, i, k):
                layernorm = pp.ln0 is not None
                t = i * pp.unroll + k
                e = k + pp.ahead - 2
                new_unit = layernorm and k % GT == 0 and inside(t + pp.ahead - 2, NT)
                unit = i * (pp.unroll // GT) + e // GT
                if new_unit:
                    scale_of(pp, unit, e % U, GT)
                if layernorm and inside(t + pp.ahead, NT):
                    q, j = (k + pp.ahead) % pp.unroll // GT, k % GT
                    if j == 0:
                        v.wait_ge(pp.x_in[q], pp.x_base + pp.x_unit * (i + (k + pp.ahead) // pp.unroll + 1))
                    v.bn_stats(stats[:, (k + pp.ahead) % U, :], pp.x[q][:, j, 0:D]).then_inc(stat, 1)
                if new_unit:
                    shift_of(pp, unit, e % U, GT,
                             pp.x[e % pp.unroll // GT][:, :, D:D + 1].rearrange("p g o -> p (g o)")
                             if pp is Z else None)
                if inside(t + 1, NT):
                    split_lower(pp, t + 1, k + 1)
                if layernorm and inside(t + pp.ahead, NT):
                    tile_moments(pp, t + pp.ahead, (k + pp.ahead) % U)
                if inside(t - 1, NT):
                    q, j = (k - 1) % pp.unroll // GT, (k - 1) % GT
                    slots = len(pp.results)
                    if j == 0:
                        wait(v, pp.stored[q % slots], pp.stored_base + pp.stored_unit * (
                            i * (len(pp.x) // slots) + (k - 1) // GT // slots))
                    v.wait_ge(product, pp.tile0 + t)
                    if pp is A:
                        addend = bias[0][:, :]
                    elif pp is C:
                        addend = pp.other[q][:, j, :]
                        v.wait_ge(g_biased, i * (U // GT) + (k - 1) // GT + 1)
                    else:
                        addend = scaled_bias[:, (k - 1) % 4, :]
                        v.wait_ge(bias_scaled, t)
                    v.scalar_tensor_tensor(out=pp.results[q % slots][:, j, 0:D], in0=psZ[:, (k - 1) % ZS, :],
                                           scalar=1.0 / SCALE, in1=addend,
                                           op0=ALU.mult, op1=ALU.add).then_inc(evac_v, 1)
                if pp is A and isinstance(i, int) and i == 0:
                    if k + A.ahead < CHUNKS:
                        pick(k + A.ahead)
                    if k == PICK_END:
                        take_records()
                    if 0 <= k - (U - KC):
                        chunk = k - (U - KC)
                        split_low_of_matrix(1, slice(chunk, chunk + 1), 1 + chunk + 1)
                if pp is A and isinstance(i, int) and i > 0 and k == 0:
                    v.wait_ge(counted, ET // SG)
                    targets(flag[:, 1, :], flag[:, 2, :], rec[:, 1, :], index[:, :, 1])
                if pp is not Z and not isinstance(i, int) and k in scale_at[pp.number]:
                    add_bases(pp.number, i, scale_at[pp.number][k])
                if pp is A and not isinstance(i, int):
                    compare(i, k)

            def edge_step(ep, i, k):
                layernorm = ep.ln0 is not None
                a = i * U + k + 4
                n = i * U + k + 3
                if layernorm and inside(n, ep.tiles):
                    scale_of(ep, n, (k + 3) % U, 1)
                if layernorm and inside(a, ep.tiles):
                    v.wait_ge(gathered[(k + 4) % GS],
                              16 * (ep.number * (ET // GS) + i * (U // GS) + (k + 4) // GS + 1))
                    v.bn_stats(stats[:, (k + 4) % U, :], rows[:, (k + 4) % GS, 0:D]).then_inc(stat, 1)
                if layernorm and inside(n, ep.tiles):
                    shift_of(ep, n, (k + 3) % U, 1)
                h = i * U + k + 1
                if inside(h, ep.tiles):
                    split_lower(ep, h, k + 1)
                if layernorm and inside(a, ep.tiles):
                    tile_moments(ep, a, (k + 4) % U)
                b = i * U + k + 2
                if inside(b, ep.tiles):
                    c = k % 2
                    weight = rows[:, (k + 2) % GS, D:D + 1] if ep is Fp else rec[:, 2, bass.ds(b, 1)]
                    v.wait_ge(rows_hi, ep.number * ET + b + 1)
                    v.scalar_tensor_tensor(out=parted[:, c, 1, :], in0=act[:, c, :], scalar=weight,
                                           in1=parted[:, c, 0, :], op0=ALU.mult, op1=ALU.subtract)\
                     .then_inc(rows_lo, 1)
                if ep is Fp and inside(b, ep.tiles):
                    wait(v, turned, ep.tile0 + b - 1)
                    v.tensor_scalar(mix[:, c % 2, :], same2[:, bass.ds(b, 1), :].rearrange("p a j -> p (a j)"),
                                    rows[:, (k + 2) % GS, D:D + 1], None, ALU.mult).then_inc(mixed, 1)
                if ep is Bp and isinstance(i, int) and i == 0 and 0 <= k < KC:
                    split_low_of_matrix(2, slice(k, k + 1), 1 + KC + k + 1)
                if ep is Bp and not isinstance(i, int):
                    count_degrees(i, k)
                if ep is Dp and not isinstance(i, int):
                    compare_dense(i, k)
                if ep is Dp and isinstance(i, int) and i > 0 and k == 0:
                    v.wait_ge(dense_counted, 2 + EC // 2)
                    link(v.tensor_copy(index2[:, :, 0], edge_f[:, 0, :]))
                    targets(earlier_count, target2, edge_f[:, 1, :], index2[:, :, 1])
                if ep is Bp and isinstance(i, int) and i > 0 and k == 3:
                    v.wait_ge(deg_std, 1)
                    v.reciprocal(dis[:, :], dis[:, :]).then_inc(graph_ready, 1)
                if ep is Fp:
                    t = i * U + k - 1
                    if inside(t, ep.tiles):
                        v.wait_ge(product, ep.tile0 + t + 1)
                        wait(v, added, 16 * (ep.number * ET + t - MS + 1))
                        v.wait_ge(bias_row, t + 1)
                        v.scalar_tensor_tensor(out=msgs[:, (k - 1) % MS, 0:D], in0=psZ[:, (k - 1) % ZS, :],
                                               scalar=1.0 / SCALE, in1=bias_rows[:, (k - 1) % 4, :],
                                               op0=ALU.mult, op1=ALU.add).then_inc(evac_v, 1)
            step_a, step_b, step_c, step_d, step_f, step_z = (
                lambda i, k, step=step, pp=pp: step(pp, i, k)
                for step, pp in ((node_step, A), (edge_step, Bp), (node_step, C), (edge_step, Dp),
                                 (edge_step, Fp), (node_step, Z)))
            steps(v, NT, U, A.ahead, step_a, tail=1, after_last=ahead_of(step_b, 4))
            v.memset(msgs[:, :, D:WIDE], 0.0).then_inc(message_ends, 1)
            v.wait_ge(split_lo, 1 + KC)
            steps(v, ET, U, 0, step_b)
            steps(v, NT, U, 1, step_c, tail=1, after_last=ahead_of(step_d, 4))
            v.sem_inc(dense_counted, 2)
            steps(v, ET, U, 0, step_d)
            steps(v, EC, U, 4, step_f, tail=1, after_last=ahead_of(step_z, Z.ahead, Z.ahead - 4))
            steps(v, NT, Z.unroll, 0, step_z, tail=1)

        @block.tensor
        def _(pe):
            pe.wait_ge(setup, 12)
            pe.wait_ge(pool_const, 6)
            pe.matmul(psZ[:, 0, 0:R], before[0:EP, :], counts[0:EP, 1, :], start=True, stop=True)
            pe.matmul(psZ[:, 1, 0:R], ones[0:EP, :], counts[0:EP, 1, :], start=True, stop=True)\
              .then_inc(setup_pe, 1)
            def pick(n):
                pe.wait_ge(picked, 3 * n + 3)
                for c in range(CH):
                    last = pe.matmul(psS[:, 0, 0:4 * ET], hotJ[n % 2][:, c, :],
                                     hotR[n % 2][:, c, :, :].rearrange("p f t -> p (f t)"),
                                     start=(n == 0 and c == 0), stop=(n == CHUNKS - 1 and c == CH - 1))
                last.then_inc(picked_used, 1)

            def multiply(pp, t, k, weights):
                pe.wait_ge(lo_done, pp.tile0 + t + 1)
                s = k % 2
                for c in range(KC):
                    for part, half in ((0, 0), (0, 1), (1, 0)):
                        last = pe.matmul(psZ[:, k % ZS, :], actT[:, s, part, c * P:(c + 1) * P], weights(half, c),
                                         start=(c == 0 and part == 0 and half == 0), stop=(c == KC - 1 and part == 1))
                last.then_inc(product, 1)

            def slot_free(pp, t, evacuated):
                if not isinstance(t, int) or t >= ZS:
                    pe.wait_ge(evacuated, pp.evac0 + t - ZS + 1)
                elif pp in last_evacuation:
                    before, count = last_evacuation[pp]
                    pe.wait_ge(before, count - ZS + 1 + t)

            last_evacuation = {Bp: (evac_v, A.evac0 + NT), C: (evac_s, Bp.evac0 + ET), Dp: (evac_v, C.evac0 + NT),
                               Fp: (evac_s, Dp.evac0 + ET), Z: (evac_v, Fp.evac0 + EC)}

            def turn_slot_free(pp, t):
                wait(pe, lo_done, pp.tile0 + t - 1)

            def node_step(pp, i, k, w):
                a = i * pp.unroll + k + 1
                if inside(a, NT):
                    c = k + 1
                    q, j = (k + 1) % pp.unroll // GT, (k + 1) % GT
                    if pp is C:
                        if j == 0:
                            pe.wait_ge(pp.x_in[q], pp.x_base + pp.x_unit * (i + (k + 1) // pp.unroll + 1))
                        source = pp.x[q][:, j, 0:D]
                    else:
                        pe.wait_ge(normed, pp.norm0 + a + 1)
                        source = act[:, c % 2, :]
                    turn_slot_free(pp, a)
                    for n in range(KC):
                        last = pe.transpose(psT[:, c % 2, n * P:(n + 1) * P], source[:, n * P:(n + 1) * P], ident[:, :])
                    last.then_inc(turned, 1)
                t = i * pp.unroll + k
                if inside(t, NT):
                    slot_free(pp, t, evac_v)
                    multiply(pp, t, k, lambda half, c: w[:, half, c, :])
                if pp is A and isinstance(i, int) and i == 0 and k < PICK_END:
                    pick(k + A.ahead - 1)
                if pp is A and not isinstance(i, int) and k in (1, 4):
                    h = (k - 1) // 3
                    pe.wait_ge(spread, 2 * (i - 1) + h + 1)
                    pe.matmul(psS[:, h, 0:SG * P], ones[:, :], diag[h].rearrange("p t j -> p (t j)"),
                              start=True, stop=True).then_inc(spread_pe, 1)

            def edge_step(ep, i, k):
                if ep is Bp and not isinstance(i, int) and k in (4, 7):
                    h = (k - 4) // 3
                    pe.wait_ge(deg_hot, 6 * (2 * (i - 1) + h + 1))
                    for c in range(CH):
                        last = pe.matmul(psS[:, h, 0:NT], hotQ[h][:, c, :], hotT[h][:, c, :],
                                         start=(c == 0), stop=(c == CH - 1))
                    last.then_inc(deg_used, 1)
                a = i * U + k + 1
                if inside(a, ep.tiles):
                    c = (k + 1) % U
                    pe.wait_ge(rows_lo, ep.number * ET + a + 1)
                    turn_slot_free(ep, a)
                    equal = ep.same[:, bass.ds(a, 1), :].rearrange("p a j -> p (a j)")
                    for n in range(KC):
                        for part in range(2):
                            last = pe.matmul(psT[:, c % 2, n * P:(n + 1) * P],
                                             parted[:, c % 2, part, n * P:(n + 1) * P], equal,
                                             start=(part == 0), stop=(part == 1))
                    if ep is Fp:
                        pe.wait_ge(mixed, a + 1)
                        wait(pe, summed, a - 1)
                        last = pe.matmul(psS[:, c % 2, 0:1], mix[:, c % 2, :], ones[:, 0:1],
                                         start=True, stop=True)
                    last.then_inc(turned, 1)
                t = i * U + k
                if inside(t, ep.tiles):
                    if ep is Fp:
                        weights = lambda half, c: node_w[0][:, half, c, :]
                    else:
                        r = pe.value_load(tile_rel[0:1, bass.ds(t, 1)], min_val=0, max_val=R - 1)
                        weights = lambda half, c: rel_w[:, bass.ds(r * (2 * KC * D) + (half * KC + c) * D, D)]
                    slot_free(ep, t, evac_v if ep is Fp else evac_s)
                    multiply(ep, t, k, weights)
                if ep is Dp and not isinstance(i, int) and 1 <= k <= DG:
                    pe.wait_ge(dense_diag, DG * (i - 1) + k)
                    pe.matmul(psS[:, (k - 1) % 2, 0:2 * P], ones[:, :], diag2[(k - 1) % 2].rearrange("p t j -> p (t j)"),
                              start=True, stop=True).then_inc(dense_pe, 1)

            pe.wait_ge(split_lo, 1)
            pe.wait_ge(placed, 1)
            step_a = lambda i, k: node_step(A, i, k, node_w[0])
            step_b = lambda i, k: edge_step(Bp, i, k)
            step_c = lambda i, k: node_step(C, i, k, node_w[1])
            step_d = lambda i, k: edge_step(Dp, i, k)
            step_f = lambda i, k: edge_step(Fp, i, k)
            step_z = lambda i, k: node_step(Z, i, k, node_w[0])
            for n in range(A.ahead - 2):
                pick(n)
            steps(pe, NT, U, 1, step_a, after_last=ahead_of(step_b, 1))
            pe.wait_ge(rel_free, BLOCKS + 2)
            pe.wait_ge(graph_ready, 1)
            steps(pe, ET, U, 0, step_b)
            pe.wait_ge(split_lo, 1 + KC)
            steps(pe, NT, U, 1, step_c, after_last=ahead_of(step_d, 1))
            pe.wait_ge(rel_free, 2 * BLOCKS + 2)
            steps(pe, ET, U, 0, step_d)
            pe.wait_ge(split_lo, 1 + 2 * KC)
            steps(pe, EC, U, 1, step_f, after_last=ahead_of(step_z, 1))
            steps(pe, NT, Z.unroll, 0, step_z)


def kernel(x, src, dst, edge_type_8, edge_weight, L0_gnn_basis0, L0_gnn_comp0, L0_gnn_bias0, L0_gnn_loop0,
           L0_gnn_basis1, L0_gnn_comp1, L0_gnn_bias1, L0_gnn_loop1, L1_gnn_W, L1_gnn_b):
    import numpy as np
    import concourse.bacc as bacc
    from concourse.bass_utils import run_bass_kernel_spmd

    nc = bacc.Bacc("TRN2", target_bir_lowering=False, num_devices=1)
    inputs = [("x", x), ("src", src), ("dst", dst), ("etype", edge_type_8), ("weight", edge_weight),
              ("basis0", L0_gnn_basis0), ("comp0", L0_gnn_comp0), ("bias0", L0_gnn_bias0), ("loop0", L0_gnn_loop0),
              ("basis1", L0_gnn_basis1), ("comp1", L0_gnn_comp1), ("bias1", L0_gnn_bias1), ("loop1", L0_gnn_loop1),
              ("w2t", np.asarray(L1_gnn_W).T), ("bias2", L1_gnn_b)]
    arrays, args = {}, []
    for name, a in inputs:
        a = np.ascontiguousarray(a)
        arrays[f"in_{name}"] = a
        args.append(nc.dram_tensor(f"in_{name}", a.shape, mybir.dt.from_np(a.dtype), kind="ExternalInput").ap())
    out = nc.dram_tensor("out_x", tuple(x.shape), F32, kind="ExternalOutput").ap()
    gnn_kernel(nc, *args, out)
    r = run_bass_kernel_spmd(nc, [arrays], core_ids=[0])
    return r.results[0]["out_x"]
```
